# Optimizing a Trainium2 kernel written in Bass

```python
import numpy as np
import jax
import jax.numpy as jnp

def _softmax(x, axis=-1):
    return jax.nn.softmax(x, axis=axis)

def _gelu(x):
    return jax.nn.gelu(x, approximate=True)

def _silu(x):
    return jax.nn.silu(x)

def _sigmoid(x):
    return jax.nn.sigmoid(x)

def _layernorm(x, axis=-1, eps=1e-05):
    m = jnp.mean(x, axis=axis, keepdims=True)
    v = jnp.var(x, axis=axis, keepdims=True)
    return (x - m) / jnp.sqrt(v + eps)

def _scatter_add(tgt, idx, src, axis=0):
    return tgt.at[idx].add(src)

def _segment_sum(src, seg, n):
    return jax.ops.segment_sum(src, seg, n)
kernel_name = 'mk_prb_d1_jaxref_r8_d4958e'

def setup_inputs(seed: int=0):
    np.random.seed(seed)
    _w = jnp.asarray

    def _L0_attn_setup():
        import jax, jax.numpy as jnp
        import numpy as np
        H = 16
        EPS_DEN = 1e-06

        def _decay_scan(x, decay, init):
            xT = jnp.moveaxis(x, 2, 0)

            def step(s, xt):
                s = decay * s + xt
                return (s, s)
            _, ys = jax.lax.scan(step, init, xT)
            return jnp.moveaxis(ys, 0, 2)

        def _phi(z):
            return jax.nn.elu(z) + 1.0

        def _reference_tuple_inner(x, w_qkv, w_out, decay_param):
            B, T, Hid = x.shape
            D = Hid // H
            qkv = x @ w_qkv
            q, k, v = jnp.split(qkv, 3, axis=-1)

            def to_bhtd(t):
                return t.reshape(B, T, H, D).transpose(0, 2, 1, 3)
            q = _phi(to_bhtd(q))
            k = _phi(to_bhtd(k))
            v = to_bhtd(v)
            decay = jax.nn.sigmoid(decay_param).reshape(1, H, 1)
            init = jnp.zeros((B, H, D), dtype=x.dtype)
            running_kv = _decay_scan(k * v, decay, init)
            running_ksum = _decay_scan(k, decay, init)
            den = jnp.clip(jnp.sum(q * running_ksum, axis=-1, keepdims=True), EPS_DEN, None)
            out = q * running_kv / den
            out = out.transpose(0, 2, 1, 3).reshape(B, T, Hid) @ w_out
            new_kv = running_kv[:, :, -1, :]
            new_ksum = running_ksum[:, :, -1, :]
            return (out, new_kv, new_ksum)
        key = jax.random.key(seed)
        k1, k2, k3 = jax.random.split(key, 3)
        x = jax.random.normal(k1, (2, 512, 256), dtype=jnp.float32)
        w_qkv = jax.random.normal(k2, (256, 768), dtype=jnp.float32) * 0.02
        w_out = jax.random.normal(k3, (256, 256), dtype=jnp.float32) * 0.02
        decay_param = jnp.full((H,), 0.95, dtype=jnp.float32)
        return {'x': x, 'w_qkv': w_qkv, 'w_out': w_out, 'decay_param': decay_param}
    _L0_attn_in = _L0_attn_setup()

    def _L0_ffn_setup():
        import jax, jax.numpy as jnp
        import numpy as np
        B, S, D, F, E, K = (2, 256, 256, 512, 8, 1)

        def _silu_mul(gu):
            g, u = jnp.split(gu, 2, axis=-1)
            return jax.nn.silu(g) * u

        def _moe_forward(hidden_states, router_w, w_gate_up, w_down, shared_gate_up, shared_down, top_k=K):
            b, s, d = hidden_states.shape
            x = hidden_states.reshape(-1, d)
            router_logits = x @ router_w.T
            topk_vals, topk_ids = jax.lax.top_k(router_logits, top_k)
            gate = jax.nn.sigmoid(topk_vals.astype(jnp.float32)).astype(x.dtype)
            xs = (x[:, None, :] * gate[:, :, None]).reshape(-1, d)
            ids_flat = topk_ids.reshape(-1)
            n_experts = w_gate_up.shape[0]

            def body(acc, inp):
                wg, wd, e = inp
                h = _silu_mul(xs @ wg)
                o = h @ wd
                mask = (ids_flat == e)[:, None]
                return (acc + jnp.where(mask, o, jnp.zeros((), o.dtype)), None)
            acc0 = jnp.zeros_like(xs)
            routed, _ = jax.lax.scan(body, acc0, (w_gate_up, w_down, jnp.arange(n_experts)))
            routed = routed.reshape(-1, top_k, d).sum(1)
            shared = _silu_mul(x @ shared_gate_up) @ shared_down
            return (routed + shared).reshape(b, s, d)
        key = jax.random.key(seed)
        ks = jax.random.split(key, 6)
        scale = 0.02
        return {'hidden_states': jax.random.normal(ks[0], (B, S, D), jnp.float32), 'router_w': jax.random.normal(ks[1], (E, D), jnp.float32) * scale, 'w_gate_up': jax.random.normal(ks[2], (E, D, 2 * F), jnp.float32) * scale, 'w_down': jax.random.normal(ks[3], (E, F, D), jnp.float32) * scale, 'shared_gate_up': jax.random.normal(ks[4], (D, 2 * F), jnp.float32) * scale, 'shared_down': jax.random.normal(ks[5], (F, D), jnp.float32) * scale}
    _L0_ffn_in = _L0_ffn_setup()
    _d = {'L0_attn_x': _L0_attn_in['x'], 'L0_attn_w_qkv': _L0_attn_in['w_qkv'], 'L0_attn_w_out': _L0_attn_in['w_out'], 'L0_attn_decay_param': _L0_attn_in['decay_param'], 'L0_ffn_router_w': _L0_ffn_in['router_w'], 'L0_ffn_w_gate_up': _L0_ffn_in['w_gate_up'], 'L0_ffn_w_down': _L0_ffn_in['w_down'], 'L0_ffn_shared_gate_up': _L0_ffn_in['shared_gate_up'], 'L0_ffn_shared_down': _L0_ffn_in['shared_down']}
    _x0 = _d['L0_attn_x']
    _d['L0_attn_x'] = jax.random.normal(jax.random.fold_in(jax.random.key(seed), 1), (1, 1024, 256), dtype=_x0.dtype)
    del _x0
    return _d

def reference(L0_attn_x, L0_attn_w_qkv, L0_attn_w_out, L0_attn_decay_param, L0_ffn_router_w, L0_ffn_w_gate_up, L0_ffn_w_down, L0_ffn_shared_gate_up, L0_ffn_shared_down):

    def _L0_attn_ref(x, w_qkv, w_out, decay_param):
        import jax, jax.numpy as jnp
        import numpy as np
        H = 16
        EPS_DEN = 1e-06

        def _decay_scan(x, decay, init):
            xT = jnp.moveaxis(x, 2, 0)

            def step(s, xt):
                s = decay * s + xt
                return (s, s)
            _, ys = jax.lax.scan(step, init, xT)
            return jnp.moveaxis(ys, 0, 2)

        def _phi(z):
            return jax.nn.elu(z) + 1.0

        def _reference_tuple_inner(x, w_qkv, w_out, decay_param):
            B, T, Hid = x.shape
            D = Hid // H
            qkv = x @ w_qkv
            q, k, v = jnp.split(qkv, 3, axis=-1)

            def to_bhtd(t):
                return t.reshape(B, T, H, D).transpose(0, 2, 1, 3)
            q = _phi(to_bhtd(q))
            k = _phi(to_bhtd(k))
            v = to_bhtd(v)
            decay = jax.nn.sigmoid(decay_param).reshape(1, H, 1)
            init = jnp.zeros((B, H, D), dtype=x.dtype)
            running_kv = _decay_scan(k * v, decay, init)
            running_ksum = _decay_scan(k, decay, init)
            den = jnp.clip(jnp.sum(q * running_ksum, axis=-1, keepdims=True), EPS_DEN, None)
            out = q * running_kv / den
            out = out.transpose(0, 2, 1, 3).reshape(B, T, Hid) @ w_out
            new_kv = running_kv[:, :, -1, :]
            new_ksum = running_ksum[:, :, -1, :]
            return (out, new_kv, new_ksum)
        return _reference_tuple_inner(x, w_qkv, w_out, decay_param)[0]

    def _L0_ffn_ref(hidden_states, router_w, w_gate_up, w_down, shared_gate_up, shared_down):
        import jax, jax.numpy as jnp
        import numpy as np
        B, S, D, F, E, K = (2, 256, 256, 512, 8, 1)

        def _silu_mul(gu):
            g, u = jnp.split(gu, 2, axis=-1)
            return jax.nn.silu(g) * u

        def _moe_forward(hidden_states, router_w, w_gate_up, w_down, shared_gate_up, shared_down, top_k=K):
            b, s, d = hidden_states.shape
            x = hidden_states.reshape(-1, d)
            router_logits = x @ router_w.T
            topk_vals, topk_ids = jax.lax.top_k(router_logits, top_k)
            gate = jax.nn.sigmoid(topk_vals.astype(jnp.float32)).astype(x.dtype)
            xs = (x[:, None, :] * gate[:, :, None]).reshape(-1, d)
            ids_flat = topk_ids.reshape(-1)
            n_experts = w_gate_up.shape[0]

            def body(acc, inp):
                wg, wd, e = inp
                h = _silu_mul(xs @ wg)
                o = h @ wd
                mask = (ids_flat == e)[:, None]
                return (acc + jnp.where(mask, o, jnp.zeros((), o.dtype)), None)
            acc0 = jnp.zeros_like(xs)
            routed, _ = jax.lax.scan(body, acc0, (w_gate_up, w_down, jnp.arange(n_experts)))
            routed = routed.reshape(-1, top_k, d).sum(1)
            shared = _silu_mul(x @ shared_gate_up) @ shared_down
            return (routed + shared).reshape(b, s, d)
        return _moe_forward(hidden_states, router_w, w_gate_up, w_down, shared_gate_up, shared_down)
    x = L0_attn_x
    xn = _layernorm(x, axis=-1)
    x = x + _L0_attn_ref(xn, L0_attn_w_qkv, L0_attn_w_out, L0_attn_decay_param) + _L0_ffn_ref(xn, L0_ffn_router_w, L0_ffn_w_gate_up, L0_ffn_w_down, L0_ffn_shared_gate_up, L0_ffn_shared_down)
    return x

_drawn_inputs = setup_inputs


def setup_inputs(seed=0):
    import zlib

    import numpy as np

    out = dict(_drawn_inputs(seed))
    spreads = {'L0_attn_decay_param': (0.949999988079071, 0.6)}
    factors = {'L0_attn_w_qkv': 23.297,
     'L0_attn_w_out': 23.071,
     'L0_ffn_router_w': 6.562,
     'L0_ffn_w_gate_up': 6.115,
     'L0_ffn_w_down': 6.098,
     'L0_ffn_shared_gate_up': 8.0,
     'L0_ffn_shared_down': 8.0}
    for name, (base, spread) in spreads.items():
        noise = np.random.default_rng([zlib.crc32(name.encode()), seed]).standard_normal(out[name].shape)
        drawn = base * np.exp(spread * noise) if base else spread * noise
        out[name] = jnp.asarray(drawn.astype(out[name].dtype))
    for name, factor in factors.items():
        out[name] = (out[name] * factor).astype(out[name].dtype)
    return out
```

```python
from contextlib import ExitStack

import concourse.bass as bass
from concourse import mybir

ALU = mybir.AluOpType
ACT = mybir.ActivationFunctionType
AX = mybir.AxisListType
F32 = mybir.dt.float32
F32R = mybir.dt.float32r
BF16 = mybir.dt.bfloat16
I32 = mybir.dt.int32

P = 128
HEADS = 16
EPS_LN = 1e-5
EPS_DEN = 1e-6
SLOTS = 160
HS = SLOTS // 2


def build(nc, x, w_qkv, w_out, decay_param, router_w, w_gate_up, w_down, shared_gate_up, shared_down, out):
    _, T, D = x.shape
    E, _, F2 = w_gate_up.shape
    F = F2 // 2
    NT = T // P
    KC = D // P
    FC = F // P
    NH = T // 512
    TH = NT // NH
    HC = HEADS // KC
    HD = D // HEADS
    TILES = (T + E * (SLOTS - 1)) // SLOTS
    STEPS = (T - 1) // SLOTS
    ROWS = (TILES + 2) * SLOTS

    x_rows = x.rearrange("a (i p) d -> p (a i) d", p=P)
    out_rows = out.rearrange("a (i p) d -> p (a i) d", p=P)
    sorted_rows = nc.dram_tensor("sorted_rows", (ROWS, D), F32, kind="Internal").ap()

    with ExitStack() as ctx:
        def sb(name, shape, dt):
            return ctx.enter_context(nc.sbuf_tensor(name, shape, dt))

        def sem(name):
            return ctx.enter_context(nc.semaphore(name))

        ident = sb("ident", [P, P], F32)
        before = sb("before", [P, P], BF16)
        ones = sb("ones", [P, P], BF16)
        head_of = sb("head_of", [P, HC], F32)
        spread = sb("spread", [HEADS, KC, P], F32)
        em = sb("em", [P, E], F32)
        em_int = sb("em_int", [P, E], I32)
        steps_int = sb("steps_int", [P, E, STEPS], I32)
        steps = sb("steps", [P, E, STEPS], F32)
        restart = sb("restart", [P, E, NT], F32)
        ones8 = sb("ones8", [P, E], F32)
        ZK = 16
        ZW = ROWS * D // P // ZK
        zeros = sb("zeros", [P, ZW], F32)
        x_sb = sb("x_sb", [P, NT, D], F32)
        xn = sb("xn", [P, NT, D], F32)
        bn = sb("bn", [P, NT, 6], F32)
        mv = sb("mv", [P, NT, 2], F32)
        ve = sb("ve", [P, NT], F32)
        sd = sb("sd", [P, NT], F32)
        rs = sb("rs", [P, NT], F32)
        rt = sb("rt", [P, NT], F32)
        rstd = sb("rstd", [P, NT], F32)
        xT_hi = sb("xT_hi", [P, KC, T], F32R)
        xT_lo = sb("xT_lo", [P, KC, T], F32R)
        router = sb("router", [E, D], F32)
        rT_hi = sb("rT_hi", [P, KC, E], F32R)
        rT_lo = sb("rT_lo", [P, KC, E], F32R)
        top = sb("top", [P, NT], F32)
        is_top = sb("is_top", [P, E, NT], F32)
        cand = sb("cand", [P, E, NT], F32)
        first = sb("first", [P, NT], F32)
        chosen = sb("chosen", [P, E, NT], BF16)
        upto = sb("upto", [P, E, NT], F32)
        pos = sb("pos", [P, E, NT], F32)
        over = sb("over", [P, E, STEPS], F32)
        tiles_of = sb("tiles_of", [P, E], F32)
        tiles_one = sb("tiles_one", [P, E], F32)
        tiles_upto = sb("tiles_upto", [P, E], F32)
        base = sb("base", [P, E], F32)
        slot = sb("slot", [P, NT], F32)
        slot_row = sb("slot_row", [P, NT], I32)
        plan = sb("plan", [1, 2 * E + 1], I32)
        gexp = sb("gexp", [P, NT], F32)
        gone = sb("gone", [P, NT], F32)
        gate = sb("gate", [P, NT], F32)
        wqkv = sb("wqkv", [P, KC, 3 * D], F32)
        wqkv_hi = sb("wqkv_hi", [P, KC, 3 * D], F32R)
        wqkv_lo = sb("wqkv_lo", [P, KC, 3 * D], F32R)
        wout = sb("wout", [P, KC, D], F32)
        dec_in = sb("dec_in", [HEADS, 1], F32)
        dec_e = sb("dec_e", [HEADS, 1], F32)
        dec_1 = sb("dec_1", [HEADS, 1], F32)
        dec_h = sb("dec_h", [HEADS, 1], F32)
        decay = sb("decay", [P, KC], F32)
        ez = sb("ez", [P, 2, 512], F32)
        rz = sb("rz", [P, 2, 512], F32)
        k_sb = sb("k_sb", [P, 512], F32)
        kv_sb = sb("kv_sb", [P, 512], F32)
        q_sb = sb("q_sb", [P, KC, T], F32)
        ksum = sb("ksum", [P, KC, T], F32)
        kvsum = sb("kvsum", [P, KC, T], F32)
        den = sb("den", [P, NT * HEADS], F32)
        rden = sb("rden", [P, NT * HEADS], F32)
        sgu = sb("sgu", [P, KC, F2], F32)
        sgu_hi = sb("sgu_hi", [P, KC, F2], F32R)
        sgu_lo = sb("sgu_lo", [P, KC, F2], F32R)
        sdn = sb("sdn", [P, FC, D], F32)
        act_sb = sb("act_sb", [P, 2, 512], F32)
        hT = [sb(f"hT{n}", [P, FC, 512], F32) for n in range(NH)]
        gu = [sb(f"gu{p}", [P, KC, F2], F32) for p in range(2)]
        gu_hi = [sb(f"gu_hi{p}", [P, KC, F2], F32R) for p in range(2)]
        gu_lo = [sb(f"gu_lo{p}", [P, KC, F2], F32R) for p in range(2)]
        dn = [sb(f"dn{p}", [P, FC, D], F32) for p in range(2)]
        early = wqkv[:, :, :].rearrange("p c n -> p (c n)")
        xg = early[0:HS, 0:2 * D].rearrange("p (j d) -> p j d", j=2)
        hr = early[:, 2 * D:2 * D + FC * SLOTS].rearrange("p (f s) -> p f s", f=FC)
        xgT_hi = sb("xgT_hi", [P, KC, SLOTS], F32R)
        xgT_lo = sb("xgT_lo", [P, KC, SLOTS], F32R)
        yT = sb("yT", [P, KC, SLOTS], F32)
        yrow = sb("yrow", [HS, 2, D], F32)
        y_tok = q_sb[:, :, :].rearrange("p c (j d) -> p (c j) d", d=D)
        rdT = ez[0:HEADS, :, :].rearrange("p a b -> p (a b)")

        ps = ctx.enter_context(nc.psum_tensor("ps", [P, 8, 512], F32))
        ROUTE = 6
        logits = ps[:, ROUTE, 0:NT * E].rearrange("p (i e) -> p e i", e=E)
        rank_ps = ps[:, ROUTE, 64:64 + NT * E]
        count_ps = ps[:, ROUTE, 128:128 + NT * E]

        s_x = [sem(f"s_x{n}") for n in range(NH)]
        s_router = sem("s_router")
        s_dec = sem("s_dec")
        s_wqkv = sem("s_wqkv")
        s_wout = sem("s_wout")
        s_sgu = sem("s_sgu")
        s_sdn = sem("s_sdn")
        s_gu = [sem(f"s_gu{p}") for p in range(2)]
        s_dn = [sem(f"s_dn{p}") for p in range(2)]
        s_zero = sem("s_zero")
        s_const = sem("s_const")
        s_ve = sem("s_ve")
        s_sd = sem("s_sd")
        s_xn = sem("s_xn")
        s_xT = sem("s_xT")
        s_rT = sem("s_rT")
        s_rhi = sem("s_rhi")
        s_rlo = sem("s_rlo")
        s_xhi = sem("s_xhi")
        s_xlo = sem("s_xlo")
        s_logit = sem("s_logit")
        s_top = sem("s_top")
        s_gexp = sem("s_gexp")
        s_chosen = sem("s_chosen")
        s_rank = sem("s_rank")
        s_slot = sem("s_slot")
        s_plan = sem("s_plan")
        s_xs = sem("s_xs")
        s_scatter = sem("s_scatter")
        s_whi = sem("s_whi")
        s_wlo = sem("s_wlo")
        s_dece = sem("s_dece")
        s_dech = sem("s_dech")
        s_decp = sem("s_decp")
        s_qkv = sem("s_qkv")
        s_er = sem("s_er")
        s_kv = sem("s_kv")
        s_q = sem("s_q")
        s_qk = sem("s_qk")
        s_den = sem("s_den")
        s_rden = sem("s_rden")
        s_rdT = sem("s_rdT")
        s_rdTc = sem("s_rdTc")
        s_spread = sem("s_spread")
        s_att = sem("s_att")
        s_shi = sem("s_shi")
        s_slo = sem("s_slo")
        s_sg = sem("s_sg")
        s_ss = sem("s_ss")
        s_sh = sem("s_sh")
        s_ghi = sem("s_ghi")
        s_glo = sem("s_glo")
        s_xg = sem("s_xg")
        s_xgT = sem("s_xgT")
        s_xghi = sem("s_xghi")
        s_xglo = sem("s_xglo")
        s_gup = sem("s_gup")
        s_silu = sem("s_silu")
        s_hr = sem("s_hr")
        s_down = sem("s_down")
        s_yT = sem("s_yT")
        s_yback = sem("s_yback")
        s_yrow = sem("s_yrow")
        s_ystore = sem("s_ystore")
        s_stored = sem("s_stored")
        s_gather = sem("s_gather")
        s_acc = sem("s_acc")
        s_sum = sem("s_sum")
        s_fin = sem("s_fin")
        s_out = sem("s_out")
        s_dve = sem("s_dve")

        block = ctx.enter_context(nc.Block())

        gu_dram = w_gate_up.rearrange("e (c p) n -> e p c n", p=P)
        dn_dram = w_down.rearrange("e (c p) n -> e p c n", p=P)

        def three(o, w_hi, w_lo, m_hi, m_lo, start, stop):
            nc.tensor.matmul(o, w_hi, m_hi, start=start, stop=False)
            nc.tensor.matmul(o, w_hi, m_lo, start=False, stop=False)
            return nc.tensor.matmul(o, w_lo, m_hi, start=False, stop=stop)

        def run_experts(eng, expert):
            expert(0, 0, None, False)
            expert(1, 1, 32, False)
            with eng.Fori(1, E // 2 - 1) as i:
                expert(2 * i, 0, 16 * i + 16, False)
                expert(2 * i + 1, 1, 16 * i + 32, False)
            expert(E - 2, 0, 16 * (E // 2), False)
            expert(E - 1, 1, None, True)

        @block.sync
        def _(sp):
            for n in range(NH):
                sp.dma_start(x_sb[:, n * TH:(n + 1) * TH, :], x_rows[:, n * TH:(n + 1) * TH, :]).then_inc(s_x[n], 16)
            sp.dma_start(router[:, :], router_w).then_inc(s_router, 16)
            sp.dma_start(dec_in[:, :], decay_param.rearrange("(h o) -> h o", o=1)).then_inc(s_dec, 16)
            sp.dma_start(wqkv[:, :, :], w_qkv.rearrange("(c p) n -> p c n", p=P)).then_inc(s_wqkv, 16)
            sp.dma_start(sgu[:, :, :], shared_gate_up.rearrange("(c p) n -> p c n", p=P)).then_inc(s_sgu, 16)
            sp.wait_ge(s_const, 1)
            sp.dma_start(sorted_rows.rearrange("r d -> (r d)").rearrange("(p k w) -> p k w", p=P, k=ZK),
                         zeros[:, :].unsqueeze(1).broadcast_to([P, ZK, ZW])).then_inc(s_zero, 16)
            for e in range(2):
                sp.dma_start(gu[e][:, :, :], gu_dram[e]).then_inc(s_gu[e], 16)
                sp.dma_start(dn[e][:, :, :], dn_dram[e]).then_inc(s_dn[e], 16)
            sp.dma_start(sdn[:, :, :], shared_down.rearrange("(c p) n -> p c n", p=P)).then_inc(s_sdn, 16)
            sp.dma_start(wout[:, :, :], w_out.rearrange("(c p) n -> p c n", p=P)).then_inc(s_wout, 16)
            sp.wait_ge(s_plan, 3)
            with sp.Fori(0, E // 2 - 1) as i:
                for p in range(2):
                    sp.wait_ge(s_ghi, 2 * i + (p + 1))
                    sp.wait_ge(s_glo, 2 * i + (p + 1))
                    sp.dma_start(gu[p][:, :, :], gu_dram[bass.ds(2 * i + (p + 2), 1)].rearrange("e p c n -> p (e c) n")).then_inc(s_gu[p], 16)
                    done = sp.value_load(plan[0:1, bass.ds(2 * i + (E + p + 1), 1)], min_val=1, max_val=TILES)
                    sp.wait_ge(s_down, done)
                    sp.dma_start(dn[p][:, :, :], dn_dram[bass.ds(2 * i + (p + 2), 1)].rearrange("e p c n -> p (e c) n")).then_inc(s_dn[p], 16)
            for i in range(NT):
                sp.wait_ge(s_fin, i + 1)
                sp.dma_start(out_rows[:, i, :], x_sb[:, i, :]).then_inc(s_out, 16)
            sp.wait_ge(s_out, 16 * NT)

        @block.gpsimd
        def _(pool):
            pool.memset(zeros[:, :], 0.0).then_inc(s_const, 1)
            pool.memset(ident[:, :], 0.0).then_inc(s_const, 1)
            pool.memset(ones[:, :], 1.0).then_inc(s_const, 1)
            pool.memset(head_of[:, :], 1.0).then_inc(s_const, 1)
            pool.memset(spread[:, :, :], 1.0).then_inc(s_const, 1)
            pool.wait_ge(s_const, 5)
            pool.affine_select(out=ident[:, :], in_=ident[:, :], compare_op=ALU.not_equal, fill=1.0,
                               base=0, pattern=[[-1, P]], channel_multiplier=1).then_inc(s_const, 1)
            pool.affine_select(out=before[:, :], in_=ones[:, :], compare_op=ALU.is_gt, fill=0.0,
                               base=0, pattern=[[1, P]], channel_multiplier=-1).then_inc(s_const, 1)
            pool.affine_select(out=head_of[:, :], in_=head_of[:, :], compare_op=ALU.is_ge, fill=0.0,
                               base=0, pattern=[[-HD, HC]], channel_multiplier=1).then_inc(s_const, 1)
            pool.affine_select(out=spread[:, :, :], in_=spread[:, :, :], compare_op=ALU.is_ge, fill=0.0,
                               base=0, pattern=[[P, KC], [1, P]], channel_multiplier=-HD).then_inc(s_const, 1)
            pool.wait_ge(s_const, 9)
            pool.affine_select(out=head_of[:, :], in_=head_of[:, :], compare_op=ALU.is_ge, fill=0.0,
                               base=HD - 1, pattern=[[HD, HC]], channel_multiplier=-1).then_inc(s_const, 1)
            pool.affine_select(out=spread[:, :, :], in_=spread[:, :, :], compare_op=ALU.is_ge, fill=0.0,
                               base=HD - 1, pattern=[[-P, KC], [-1, P]], channel_multiplier=HD).then_inc(s_const, 1)
            pool.iota(em_int[:, :], pattern=[[1, E]], base=-E, channel_multiplier=0).then_inc(s_const, 1)
            pool.iota(steps_int[:, :, :], pattern=[[0, E], [SLOTS, STEPS]], base=SLOTS,
                      channel_multiplier=0).then_inc(s_const, 1)
            pool.memset(restart[:, :, :], 1.0).then_inc(s_const, 1)
            pool.memset(ones8[:, :], 1.0).then_inc(s_const, 1)
            pool.memset(yT[:, :, :], 0.0).then_inc(s_yT, 1)
            pool.memset(yrow[:, :, :], 0.0).then_inc(s_yrow, 1)
            pool.wait_ge(s_const, 15)
            pool.memset(restart[:, :, 0:1], 0.0).then_inc(s_const, 1)
            pool.tensor_copy(em[:, :], em_int[:, :]).then_inc(s_const, 1)
            pool.tensor_copy(steps[:, :, :], steps_int[:, :, :]).then_inc(s_const, 1)
            pool.wait_ge(s_zero, 16)
            pool.wait_ge(s_yrow, 1)
            pool.dma_start(sorted_rows[0:SLOTS, :].rearrange("(j p) d -> p j d", p=HS), yrow[:, :, :]).then_inc(s_ystore, 16)

            pool.wait_ge(s_slot, 1)
            pool.wait_ge(s_zero, 16)
            pool.wait_ge(s_ystore, 16)
            for i in range(NT):
                pool.wait_ge(s_xs, i + 1)
                pool.indirect_dma_start(sorted_rows, bass.IndirectOffsetOnAxis(ap=slot_row[:, i:i + 1], axis=0),
                                        xn[:, i, :], None).then_inc(s_scatter, 16)
            pool.wait_ge(s_scatter, 16 * NT)
            pool.dma_start(xg[:, :, :], sorted_rows[SLOTS:2 * SLOTS, :].rearrange("(j p) d -> p j d", p=HS)).then_inc(s_xg, 16)
            pool.wait_ge(s_plan, 3)
            total = pool.value_load(plan[0:1, 2 * E:2 * E + 1], min_val=E, max_val=TILES)
            with pool.Fori(0, total) as t:
                pool.wait_ge(s_xgT, t + 1)
                pool.dma_start(xg[:, :, :], sorted_rows[bass.ds(t * SLOTS + 2 * SLOTS, SLOTS), :].rearrange("(j p) d -> p j d", p=HS)).then_inc(s_xg, 16)
                pool.wait_ge(s_yrow, t + 2)
                pool.dma_start(sorted_rows[bass.ds(t * SLOTS, SLOTS), :].rearrange("(j p) d -> p j d", p=HS), yrow[:, :, :]).then_inc(s_ystore, 16)
            pool.wait_ge(s_yrow, total + 2)
            pool.dma_start(sorted_rows[bass.ds(total * SLOTS, SLOTS), :].rearrange("(j p) d -> p j d", p=HS), yrow[:, :, :]).then_inc(s_ystore, 16)
            pool.wait_ge(s_ystore, 16 * total + 32)
            pool.sem_inc(s_stored, 1)
            pool.wait_ge(s_stored, 1)
            pool.wait_ge(s_att, 4)
            for i in range(NT):
                pool.indirect_dma_start(y_tok[:, i, :], None, sorted_rows,
                                        bass.IndirectOffsetOnAxis(ap=slot_row[:, i:i + 1], axis=0)).then_inc(s_gather, 16)
            pool.wait_ge(s_gather, 16 * NT)
            pool.wait_ge(s_xg, 16 * total + 16)

        @block.scalar
        def _(act):
            def split_hi(e_done, p):
                act.wait_ge(s_gu[p], e_done)
                nc.scalar.activation(gu_hi[p][:, 0, :], gu[p][:, 0, :], ACT.Copy)
                nc.scalar.activation(gu_hi[p][:, 1, :], gu[p][:, 1, :], ACT.Copy).then_inc(s_ghi, 1)

            for n in range(NH):
                act.wait_ge(s_ve, n + 1)
                nc.scalar.activation(sd[:, n * TH:(n + 1) * TH], ve[:, n * TH:(n + 1) * TH], ACT.Sqrt).then_inc(s_sd, 1)
            act.wait_ge(s_rT, 1)
            nc.scalar.activation(rT_hi[:, :, :], ps[:, 7, 0:KC * E].rearrange("p (c e) -> p c e", e=E), ACT.Copy).then_inc(s_rhi, 1)
            for n in range(NH):
                act.wait_ge(s_xT, TH * (n + 1))
                for c in range(KC):
                    nc.scalar.activation(xT_hi[:, c, n * 512:(n + 1) * 512], ps[:, 2 * n + c, :], ACT.Copy).then_inc(s_xhi, 1)
            act.wait_ge(s_wqkv, 16)
            for j in (1, 2, 0):
                nc.scalar.activation(wqkv_hi[:, :, j * D:(j + 1) * D], wqkv[:, :, j * D:(j + 1) * D], ACT.Copy).then_inc(s_whi, 1)
            act.wait_ge(s_dec, 16)
            nc.scalar.activation(dec_e[:, :], dec_in[:, :], ACT.Exp, scale=-1.0).then_inc(s_dece, 1)
            act.wait_ge(s_top, 1)
            nc.scalar.activation(gexp[:, :], top[:, :], ACT.Exp, scale=-1.0).then_inc(s_gexp, 1)
            act.wait_ge(s_sgu, 16)
            for a in range(2 * NH):
                for j, t in ((0, 3 * a), (1, 3 * a + 2)):
                    act.wait_ge(s_qkv, t + 1)
                    if a >= 1:
                        act.wait_ge((s_kv, s_q)[j], a)
                    nc.scalar.activation(ez[:, j, :], ps[:, t % 4, :], ACT.Exp)
                    nc.scalar.activation(rz[:, j, :], ps[:, t % 4, :], ACT.Relu).then_inc(s_er, 1)
                c, h = a // 2, a % 2
                nc.scalar.activation(sgu_hi[:, c, h * F:(h + 1) * F], sgu[:, c, h * F:(h + 1) * F], ACT.Copy).then_inc(s_shi, 1)
            split_hi(16, 0)

            def shared_silu(n):
                for f in range(FC):
                    k = n * FC + f
                    act.wait_ge(s_sg, 2 * k + 1)
                    if k >= 2:
                        act.wait_ge(s_sh, k - 1)
                    nc.scalar.activation(act_sb[:, k % 2, :], ps[:, 2 * (k % 2), :], ACT.Silu).then_inc(s_ss, 1)

            shared_silu(0)
            act.wait_ge(s_rdT, 1)
            for h in range(2):
                nc.scalar.activation(rdT[:, h * 512:(h + 1) * 512], ps[0:HEADS, 6 + h, :], ACT.Copy).then_inc(s_rdTc, 1)
            act.wait_ge(s_xgT, 1)
            nc.scalar.activation(xgT_hi[:, :, :], ps[:, 4, 0:KC * SLOTS].rearrange("p (c s) -> p c s", c=KC), ACT.Copy).then_inc(s_xghi, 1)
            act.wait_ge(s_plan, 3)

            def expert(e, p, landed, last):
                start = act.value_load(plan[0:1, bass.ds(e + E, 1)], min_val=0, max_val=TILES)
                if not last:
                    if landed is not None:
                        act.wait_ge(s_down, start)
                    split_hi(landed if landed is not None else 16, 1 - p)
                count = act.value_load(plan[0:1, bass.ds(e, 1)], min_val=1, max_val=TILES)
                with act.Fori(0, count) as j:
                    t = start + j
                    for h in range(2):
                        act.wait_ge(s_gup, 2 * t + (h + 1))
                        nc.scalar.activation(act_sb[:, h, 0:2 * SLOTS], ps[:, 2 * h, 0:2 * SLOTS], ACT.Silu).then_inc(s_silu, 1)
                    act.wait_ge(s_xgT, t + 2)
                    nc.scalar.activation(xgT_hi[:, :, :], ps[:, 4, 0:KC * SLOTS].rearrange("p (c s) -> p c s", c=KC), ACT.Copy).then_inc(s_xghi, 1)
                    act.wait_ge(s_down, t + 1)
                    nc.scalar.activation(yT[:, :, :], ps[:, 5:7, 0:SLOTS], ACT.Copy).then_inc(s_yT, 1)

            run_experts(act, expert)
            shared_silu(1)

        @block.vector
        def _(dve):
            steps_done = [0]

            def link(ins):
                steps_done[0] += 1
                ins.then_inc(s_dve, 1)
                dve.wait_ge(s_dve, steps_done[0])

            V = nc.vector

            def split_lo(e_done, p):
                dve.wait_ge(s_gu[p], e_done)
                V.tensor_tensor(gu_lo[p][:, 0, :], gu[p][:, 0, :], gu_hi[p][:, 0, :].bitcast(F32), ALU.subtract)
                V.tensor_tensor(gu_lo[p][:, 1, :], gu[p][:, 1, :], gu_hi[p][:, 1, :].bitcast(F32), ALU.subtract).then_inc(s_glo, 1)

            for n in range(NH):
                dve.wait_ge(s_x[n], 16)
                h = slice(n * TH, (n + 1) * TH)
                for i in range(n * TH, (n + 1) * TH):
                    ins = V.bn_stats(bn[:, i, :], x_sb[:, i, :])
                link(ins)
                for i in range(n * TH, (n + 1) * TH):
                    ins = V.bn_aggr(mv[:, i, :], bn[:, i, :])
                link(ins)
                V.tensor_scalar(ve[:, h], mv[:, h, 1], EPS_LN, None, ALU.add).then_inc(s_ve, 1)
                dve.wait_ge(s_sd, n + 1)
                link(V.reciprocal(rs[:, h], sd[:, h]))
                link(V.tensor_tensor(rt[:, h], rs[:, h], rs[:, h], ALU.mult))
                link(V.tensor_tensor(rt[:, h], rt[:, h], ve[:, h], ALU.mult))
                link(V.tensor_scalar(rt[:, h], rt[:, h], -0.5, 1.5, ALU.mult, ALU.add))
                link(V.tensor_tensor(rstd[:, h], rs[:, h], rt[:, h], ALU.mult))
                for i in range(n * TH, (n + 1) * TH):
                    V.tensor_scalar(xn[:, i, :], x_sb[:, i, :], mv[:, i, 0:1], rstd[:, i:i + 1], ALU.subtract, ALU.mult).then_inc(s_xn, 1)
            dve.wait_ge(s_rhi, 1)
            V.tensor_tensor(rT_lo[:, :, :], ps[:, 7, 0:KC * E].rearrange("p (c e) -> p c e", e=E),
                            rT_hi[:, :, :].bitcast(F32), ALU.subtract).then_inc(s_rlo, 1)
            for n in range(NH):
                for c in range(KC):
                    dve.wait_ge(s_xhi, 2 * n + c + 1)
                    cols = slice(n * 512, (n + 1) * 512)
                    V.tensor_tensor(xT_lo[:, c, cols], ps[:, 2 * n + c, :], xT_hi[:, c, cols].bitcast(F32), ALU.subtract).then_inc(s_xlo, 1)
            for k, j in enumerate((1, 2, 0)):
                dve.wait_ge(s_whi, k + 1)
                cols = slice(j * D, (j + 1) * D)
                V.tensor_tensor(wqkv_lo[:, :, cols], wqkv[:, :, cols], wqkv_hi[:, :, cols].bitcast(F32), ALU.subtract).then_inc(s_wlo, 1)

            dve.wait_ge(s_logit, 1)
            V.tensor_reduce(top[:, :], logits.rearrange("p e i -> p i e"), AX.X, ALU.max).then_inc(s_top, 1)
            dve.wait_ge(s_top, 1)
            link(V.tensor_tensor(is_top[:, :, :], logits, top[:, :].unsqueeze(1).broadcast_to([P, E, NT]), ALU.is_equal))
            dve.wait_ge(s_const, 18)
            em_b = em[:, :].unsqueeze(2).broadcast_to([P, E, NT])
            link(V.tensor_tensor(cand[:, :, :], is_top[:, :, :], em_b, ALU.mult))
            link(V.tensor_reduce(first[:, :], cand[:, :, :].rearrange("p e i -> p i e"), AX.X, ALU.min))
            V.tensor_tensor(chosen[:, :, :], em_b, first[:, :].unsqueeze(1).broadcast_to([P, E, NT]), ALU.is_equal).then_inc(s_chosen, 1)
            dve.wait_ge(s_gexp, 1)
            link(V.tensor_scalar(gone[:, :], gexp[:, :], 1.0, None, ALU.add))
            link(V.reciprocal(gate[:, :], gone[:, :]))
            dve.wait_ge(s_dece, 1)
            link(V.tensor_scalar(dec_1[:, :], dec_e[:, :], 1.0, None, ALU.add))
            V.reciprocal(dec_h[:, :], dec_1[:, :]).then_inc(s_dech, 1)
            dve.wait_ge(s_rank, 1)
            flat = "p e i -> p (e i)"
            link(V.tensor_tensor_scan(upto[:, :, :].rearrange(flat), restart[:, :, :].rearrange(flat), count_ps, 0.0, ALU.mult, ALU.add))
            link(V.tensor_tensor(pos[:, :, :].rearrange(flat), upto[:, :, :].rearrange(flat), count_ps, ALU.subtract))
            link(V.tensor_tensor(pos[:, :, :].rearrange(flat), pos[:, :, :].rearrange(flat), rank_ps, ALU.add))
            link(V.tensor_tensor(over[:, :, :], upto[:, :, NT - 1:NT].broadcast_to([P, E, STEPS]), steps[:, :, :], ALU.is_gt))
            link(V.tensor_reduce(tiles_of[:, :], over[:, :, :], AX.X, ALU.add))
            link(V.tensor_scalar(tiles_one[:, :], tiles_of[:, :], 1.0, None, ALU.add))
            link(V.tensor_tensor_scan(tiles_upto[:, :], ones8[:, :], tiles_one[:, :], 0.0, ALU.mult, ALU.add))
            link(V.tensor_tensor(base[:, :], tiles_upto[:, :], tiles_one[:, :], ALU.subtract))
            link(V.scalar_tensor_tensor(pos[:, :, :], base[:, :].unsqueeze(2).broadcast_to([P, E, NT]), float(SLOTS), pos[:, :, :], ALU.mult, ALU.add))
            link(V.tensor_tensor(pos[:, :, :], pos[:, :, :], chosen[:, :, :], ALU.mult))
            link(V.tensor_reduce(slot[:, :], pos[:, :, :].rearrange("p e i -> p i e"), AX.X, ALU.add))
            V.tensor_scalar(slot_row[:, :], slot[:, :], float(SLOTS), None, ALU.add).then_inc(s_slot, 1)
            V.tensor_copy(plan[0:1, 0:E], tiles_one[0:1, :]).then_inc(s_plan, 1)
            V.tensor_copy(plan[0:1, E:2 * E], base[0:1, :]).then_inc(s_plan, 1)
            V.tensor_copy(plan[0:1, 2 * E:2 * E + 1], tiles_upto[0:1, E - 1:E]).then_inc(s_plan, 1)
            for i in range(NT):
                V.tensor_scalar(xn[:, i, :], xn[:, i, :], gate[:, i:i + 1], None, ALU.mult).then_inc(s_xs, 1)
            dve.wait_ge(s_decp, 1)
            link(V.tensor_copy(decay[:, :], ps[:, 7, 64:64 + KC]))

            for a in range(2 * NH):
                n, c = a // 2, a % 2
                cols = slice(n * 512, (n + 1) * 512)
                rate = decay[:, c:c + 1].broadcast_to([P, 512])
                dve.wait_ge(s_er, 2 * a + 1)
                link(V.scalar_tensor_tensor(k_sb[:, :], ez[:, 0, :], 1.0, rz[:, 0, :], ALU.min, ALU.add))
                dve.wait_ge(s_qkv, 3 * a + 2)
                V.tensor_tensor(kv_sb[:, :], k_sb[:, :], ps[:, (3 * a + 1) % 4, :], ALU.mult).then_inc(s_kv, 1)
                V.tensor_tensor_scan(ksum[:, c, cols], rate, k_sb[:, :], ksum[:, c, n * 512 - 1:n * 512] if n else 0.0, ALU.mult, ALU.add)
                dve.wait_ge(s_kv, a + 1)
                link(V.tensor_tensor_scan(kvsum[:, c, cols], rate, kv_sb[:, :], kvsum[:, c, n * 512 - 1:n * 512] if n else 0.0, ALU.mult, ALU.add))
                dve.wait_ge(s_er, 2 * a + 2)
                V.scalar_tensor_tensor(q_sb[:, c, cols], ez[:, 1, :], 1.0, rz[:, 1, :], ALU.min, ALU.add).then_inc(s_q, 1)
                dve.wait_ge(s_shi, a + 1)
                cc, h = a // 2, a % 2
                V.tensor_tensor(sgu_lo[:, cc, h * F:(h + 1) * F], sgu[:, cc, h * F:(h + 1) * F],
                                sgu_hi[:, cc, h * F:(h + 1) * F].bitcast(F32), ALU.subtract).then_inc(s_slo, 1)
            dve.wait_ge(s_q, 2 * NH)
            for c in range(KC):
                V.tensor_tensor(ksum[:, c, :], q_sb[:, c, :], ksum[:, c, :], ALU.mult).then_inc(s_qk, 1)

            def shared_hidden(n, f):
                k = n * FC + f
                dve.wait_ge(s_ss, k + 1)
                dve.wait_ge(s_sg, 2 * k + 2)
                V.tensor_tensor(hT[n][:, f, :], act_sb[:, k % 2, :], ps[:, 2 * (k % 2) + 1, :], ALU.mult).then_inc(s_sh, 1)

            shared_hidden(0, 0)
            link(V.tensor_tensor(kvsum[:, 0, :], q_sb[:, 0, :], kvsum[:, 0, :], ALU.mult))
            shared_hidden(0, 1)
            link(V.tensor_tensor(kvsum[:, 1, :], q_sb[:, 1, :], kvsum[:, 1, :], ALU.mult))
            shared_hidden(0, 2)
            dve.wait_ge(s_ghi, 1)
            split_lo(16, 0)
            shared_hidden(0, 3)
            dve.wait_ge(s_den, 1)
            link(V.tensor_scalar(den[:, :], ps[:, ROUTE, 0:NT * HEADS], EPS_DEN, None, ALU.max))
            V.reciprocal(rden[:, :], den[:, :]).then_inc(s_rden, 1)
            dve.wait_ge(s_xghi, 1)
            V.tensor_tensor(xgT_lo[:, :, :], ps[:, 4, 0:KC * SLOTS].rearrange("p (c s) -> p c s", c=KC),
                            xgT_hi[:, :, :].bitcast(F32), ALU.subtract).then_inc(s_xglo, 1)
            for c in range(KC):
                for n in range(NH):
                    dve.wait_ge(s_spread, 2 * c + n + 1)
                    cols = slice(n * 512, (n + 1) * 512)
                    V.tensor_tensor(kvsum[:, c, cols], kvsum[:, c, cols], ps[:, 2 * c + n, :], ALU.mult).then_inc(s_att, 1)

            def expert(e, p, landed, last):
                start = dve.value_load(plan[0:1, bass.ds(e + E, 1)], min_val=0, max_val=TILES)
                if not last:
                    if landed is not None:
                        dve.wait_ge(s_down, start)
                    dve.wait_ge(s_ghi, e + 2)
                    split_lo(landed if landed is not None else 16, 1 - p)
                count = dve.value_load(plan[0:1, bass.ds(e, 1)], min_val=1, max_val=TILES)
                with dve.Fori(0, count) as j:
                    t = start + j
                    dve.wait_ge(s_silu, 2 * t + 1)
                    V.tensor_tensor(hr[:, 0:2, :].rearrange("p f s -> p (f s)"), act_sb[:, 0, 0:2 * SLOTS], ps[:, 1, 0:2 * SLOTS], ALU.mult).then_inc(s_hr, 1)
                    dve.wait_ge(s_yback, t + 1)
                    dve.wait_ge(s_ystore, 16 * t + 16)
                    V.tensor_copy(yrow[:, :, :].rearrange("p j d -> p (j d)"), ps[0:HS, 7, :]).then_inc(s_yrow, 1)
                    dve.wait_ge(s_silu, 2 * t + 2)
                    V.tensor_tensor(hr[:, 2:4, :].rearrange("p f s -> p (f s)"), act_sb[:, 1, 0:2 * SLOTS], ps[:, 3, 0:2 * SLOTS], ALU.mult).then_inc(s_hr, 1)
                    dve.wait_ge(s_xghi, t + 2)
                    V.tensor_tensor(xgT_lo[:, :, :], ps[:, 4, 0:KC * SLOTS].rearrange("p (c s) -> p c s", c=KC),
                                    xgT_hi[:, :, :].bitcast(F32), ALU.subtract).then_inc(s_xglo, 1)

            dve.wait_ge(s_plan, 3)
            run_experts(dve, expert)
            total = dve.value_load(plan[0:1, 2 * E:2 * E + 1], min_val=E, max_val=TILES)
            dve.wait_ge(s_yback, total + 1)
            dve.wait_ge(s_ystore, 16 * total + 16)
            V.tensor_copy(yrow[:, :, :].rearrange("p j d -> p (j d)"), ps[0:HS, 7, :]).then_inc(s_yrow, 1)
            for f in range(FC):
                shared_hidden(1, f)
            dve.wait_ge(s_gather, 16 * NT)
            for i in range(NT):
                V.tensor_tensor(x_sb[:, i, :], x_sb[:, i, :], y_tok[:, i, :], ALU.add).then_inc(s_sum, 1)
            for i in range(NT):
                dve.wait_ge(s_acc, i + 1)
                dve.wait_ge(s_sum, i + 1)
                V.tensor_tensor(x_sb[:, i, :], x_sb[:, i, :], ps[:, 4 + i % TH, 0:D], ALU.add).then_inc(s_fin, 1)

        @block.tensor
        def _(pe):
            mm = nc.tensor.matmul
            tr = nc.tensor.transpose
            pe.wait_ge(s_const, 11)
            pe.wait_ge(s_router, 16)
            for c in range(KC):
                ins = tr(ps[:, 7, c * E:(c + 1) * E], router[:, c * P:(c + 1) * P], ident[0:E, 0:E])
            ins.then_inc(s_rT, 1)
            for i in range(NT):
                n, j = i // TH, i % TH
                pe.wait_ge(s_xn, i + 1)
                for c in range(KC):
                    ins = tr(ps[:, 2 * n + c, j * P:(j + 1) * P], xn[:, i, c * P:(c + 1) * P], ident[:, :])
                ins.then_inc(s_xT, 1)
            pe.wait_ge(s_rlo, 1)
            for i in range(NT):
                if i % TH == 0:
                    pe.wait_ge(s_xlo, 2 * (i // TH) + 2)
                cols = slice(i * P, (i + 1) * P)
                for c in range(KC):
                    ins = three(ps[:, ROUTE, i * E:(i + 1) * E], xT_hi[:, c, cols], xT_lo[:, c, cols],
                                rT_hi[:, c, :], rT_lo[:, c, :], c == 0, c == KC - 1)
            ins.then_inc(s_logit, 1)
            for t in range(6 * NH):
                a, j = t // 3, (1, 2, 0)[t % 3]
                n, c = a // 2, a % 2
                pe.wait_ge(s_wlo, min(t + 1, 3))
                if t >= 4:
                    u = t - 4
                    if u % 3 == 1:
                        pe.wait_ge(s_kv, u // 3 + 1)
                    else:
                        pe.wait_ge(s_er, 2 * (u // 3) + (1 if u % 3 == 0 else 2))
                for kc in range(KC):
                    col = j * D + c * P
                    ins = three(ps[:, t % 4, :], wqkv_hi[:, kc, col:col + P], wqkv_lo[:, kc, col:col + P],
                                xT_hi[:, kc, n * 512:(n + 1) * 512], xT_lo[:, kc, n * 512:(n + 1) * 512], kc == 0, kc == KC - 1)
                ins.then_inc(s_qkv, 1)
                if t == 1:
                    pe.wait_ge(s_chosen, 1)
                    pick = chosen[:, :, :].rearrange("p e i -> p (e i)")
                    mm(rank_ps, before[:, :], pick, start=True, stop=True)
                    mm(count_ps, ones[:, :], pick, start=True, stop=True).then_inc(s_rank, 1)
                    pe.wait_ge(s_dech, 1)
                    for c2 in range(KC):
                        ins = mm(ps[:, 7, 64 + c2:65 + c2], spread[:, c2, :], dec_h[:, :], start=True, stop=True)
                    ins.then_inc(s_decp, 1)

            def shared_gate_up_tiles(n):
                for f in range(FC):
                    k = n * FC + f
                    for u in range(2):
                        if k == 0 and u == 0:
                            pe.wait_ge(s_er, 4 * NH)
                            pe.wait_ge(s_kv, 2 * NH)
                            pe.wait_ge(s_slo, 4)
                        if k >= 2:
                            pe.wait_ge((s_ss, s_sh)[u], k - 1)
                        for kc in range(KC):
                            col = u * F + f * P
                            ins = three(ps[:, 2 * (k % 2) + u, :], sgu_hi[:, kc, col:col + P], sgu_lo[:, kc, col:col + P],
                                        xT_hi[:, kc, n * 512:(n + 1) * 512], xT_lo[:, kc, n * 512:(n + 1) * 512], kc == 0, kc == KC - 1)
                        ins.then_inc(s_sg, 1)

            def transpose_sorted(loaded):
                pe.wait_ge(s_xg, loaded)
                for c in range(KC):
                    for j in range(2):
                        col = c * SLOTS + j * HS
                        ins = tr(ps[:, 4, col:col + HS], xg[:, j, c * P:(c + 1) * P], ident[0:HS, 0:HS])
                ins.then_inc(s_xgT, 1)

            def transpose_back(copied):
                pe.wait_ge(s_yT, copied)
                for c in range(KC):
                    for j in range(2):
                        ins = tr(ps[0:HS, 7, j * D + c * P:j * D + (c + 1) * P], yT[:, c, j * HS:(j + 1) * HS], ident[:, :])
                ins.then_inc(s_yback, 1)

            shared_gate_up_tiles(0)
            pe.wait_ge(s_qk, KC)
            for i in range(NT):
                for c in range(KC):
                    col = i * HEADS + c * HC
                    ins = mm(ps[:, ROUTE, col:col + HC], ksum[:, c, i * P:(i + 1) * P], head_of[:, :], start=True, stop=True)
            ins.then_inc(s_den, 1)
            transpose_sorted(16)
            pe.wait_ge(s_rden, 1)
            for i in range(NT):
                ins = mm(ps[0:HEADS, 6 + i // 4, (i % 4) * P:(i % 4 + 1) * P], rden[:, i * HEADS:(i + 1) * HEADS], ident[:, :], start=True, stop=True)
            ins.then_inc(s_rdT, 1)
            pe.wait_ge(s_sh, FC)
            for c in range(KC):
                for n in range(NH):
                    pe.wait_ge(s_rdTc, n + 1)
                    mm(ps[:, 2 * c + n, :], spread[:, c, :], rdT[:, n * 512:(n + 1) * 512], start=True, stop=True).then_inc(s_spread, 1)
            pe.wait_ge(s_plan, 3)

            def expert(e, p, landed, last):
                pe.wait_ge(s_glo, e + 1)
                count = pe.value_load(plan[0:1, bass.ds(e, 1)], min_val=1, max_val=TILES)
                start = pe.value_load(plan[0:1, bass.ds(e + E, 1)], min_val=0, max_val=TILES)
                with pe.Fori(0, count) as j:
                    t = start + j
                    pe.wait_ge(s_xglo, t + 1)
                    for h in range(2):
                        pe.wait_ge(s_att, 2 * h + 2)
                        for u in range(2):
                            for f in (2 * h, 2 * h + 1):
                                for kc in range(KC):
                                    col = u * F + f * P
                                    ins = three(ps[:, 2 * h + u, (f % 2) * SLOTS:(f % 2 + 1) * SLOTS],
                                                gu_hi[p][:, kc, col:col + P], gu_lo[p][:, kc, col:col + P],
                                                xgT_hi[:, kc, :], xgT_lo[:, kc, :], kc == 0, kc == KC - 1)
                        ins.then_inc(s_gup, 1)
                        if h == 0:
                            pe.wait_ge(s_yrow, t + 1)
                            transpose_back(t + 1)
                    transpose_sorted(16 * t + 32)
                    pe.wait_ge(s_dn[p], dn_landed(e, p))
                    for h in range(2):
                        pe.wait_ge(s_hr, 2 * t + (h + 1))
                        for c in range(KC):
                            for f in (2 * h, 2 * h + 1):
                                ins = mm(ps[:, 5 + c, 0:SLOTS], dn[p][:, f, c * P:(c + 1) * P], hr[:, f, :],
                                         start=(f == 0), stop=(f == FC - 1))
                    ins.then_inc(s_down, 1)

            def dn_landed(e, p):
                return 8 * (e - p) + 16

            run_experts(pe, expert)
            total = pe.value_load(plan[0:1, 2 * E:2 * E + 1], min_val=E, max_val=TILES)
            pe.wait_ge(s_yrow, total + 1)
            transpose_back(total + 1)

            def finish(n):
                for i in range(n * TH, (n + 1) * TH):
                    j = i % TH
                    if n:
                        pe.wait_ge(s_fin, i - TH + 1)
                    elif j == TH - 1:
                        pe.wait_ge(s_yrow, total + 2)
                    o = ps[:, 4 + j, 0:D]
                    for f in range(FC):
                        mm(o, hT[n][:, f, j * P:(j + 1) * P], sdn[:, f, :], start=(f == 0), stop=False)
                    for c in range(KC):
                        ins = mm(o, kvsum[:, c, i * P:(i + 1) * P], wout[:, c, :], start=False, stop=(c == KC - 1))
                    ins.then_inc(s_acc, 1)

            pe.wait_ge(s_sdn, 16)
            pe.wait_ge(s_wout, 16)
            pe.wait_ge(s_xglo, total + 1)
            finish(0)
            shared_gate_up_tiles(1)
            pe.wait_ge(s_sh, 2 * FC)
            finish(1)


_INS = ['L0_attn_x', 'L0_attn_w_qkv', 'L0_attn_w_out', 'L0_attn_decay_param', 'L0_ffn_router_w', 'L0_ffn_w_gate_up',
        'L0_ffn_w_down', 'L0_ffn_shared_gate_up', 'L0_ffn_shared_down']
_OUTS = [((1, 1024, 256), 'float32')]


def kernel(**inputs):
    import numpy as _np
    import concourse.bacc as _bacc
    from concourse import mybir as _mybir
    from concourse.bass_utils import run_bass_kernel_spmd as _run

    nc = _bacc.Bacc("TRN2", target_bir_lowering=False, num_devices=1)
    arrays, args = {}, []
    for name in _INS:
        a = _np.ascontiguousarray(inputs[name])
        arrays[f"in_{name}_dram"] = a
        args.append(nc.dram_tensor(f"in_{name}_dram", a.shape, _mybir.dt.from_np(a.dtype), kind="ExternalInput").ap())
    for i, (shape, dtype) in enumerate(_OUTS):
        dt = _mybir.dt.from_np(_np.dtype(dtype))
        args.append(nc.dram_tensor(f"out_{i}_dram", shape, dt, kind="ExternalOutput").ap())
    build(nc, *args)
    r = _run(nc, [arrays], core_ids=[0])
    return r.results[0]["out_0_dram"]
```

```python
from contextlib import ExitStack

import concourse.bass as bass
from concourse import mybir

ALU = mybir.AluOpType
ACT = mybir.ActivationFunctionType
AX = mybir.AxisListType
F32 = mybir.dt.float32
F32R = mybir.dt.float32r
BF16 = mybir.dt.bfloat16
I32 = mybir.dt.int32

P = 128
HEADS = 16
EPS_LN = 1e-5
EPS_DEN = 1e-6
SLOTS = 144
HS = SLOTS // 2


def build(nc, x, w_qkv, w_out, decay_param, router_w, w_gate_up, w_down, shared_gate_up, shared_down, out):
    _, T, D = x.shape
    E, _, F2 = w_gate_up.shape
    F = F2 // 2
    NT = T // P
    KC = D // P
    FC = F // P
    NH = T // 512
    TH = NT // NH
    HC = HEADS // KC
    HD = D // HEADS
    TILES = (T + E * (SLOTS - 1)) // SLOTS
    STEPS = (T - 1) // SLOTS
    ROWS = (TILES + 2) * SLOTS

    x_rows = x.rearrange("a (i p) d -> p (a i) d", p=P)
    out_rows = out.rearrange("a (i p) d -> p (a i) d", p=P)
    sorted_rows = nc.dram_tensor("sorted_rows", (ROWS, D), F32, kind="Internal").ap()
    rden_rows = nc.dram_tensor("rden_rows", (NT * HEADS, P), F32, kind="Internal").ap()

    with ExitStack() as ctx:
        def sb(name, shape, dt):
            return ctx.enter_context(nc.sbuf_tensor(name, shape, dt))

        def sem(name):
            return ctx.enter_context(nc.semaphore(name))

        ident = sb("ident", [P, P], F32)
        before = sb("before", [P, P], BF16)
        ones = sb("ones", [P, P], BF16)
        head_of = sb("head_of", [P, HC], F32)
        spread = sb("spread", [HEADS, KC, P], F32)
        em = sb("em", [P, E], F32)
        em_int = sb("em_int", [P, E], I32)
        steps_int = sb("steps_int", [P, E, STEPS], I32)
        steps = sb("steps", [P, E, STEPS], F32)
        restart = sb("restart", [P, E, NT], F32)
        ones8 = sb("ones8", [P, E], F32)
        ZK = 16
        ZW = ROWS * D // P // ZK
        zeros = sb("zeros", [P, ZW], F32)
        x_sb = sb("x_sb", [P, NT, D], F32)
        xn = sb("xn", [P, NT, D], F32)
        bn = sb("bn", [P, NT, 6], F32)
        mv = sb("mv", [P, NT, 2], F32)
        ve = sb("ve", [P, NT], F32)
        sd = sb("sd", [P, NT], F32)
        rs = sb("rs", [P, NT], F32)
        rt = sb("rt", [P, NT], F32)
        rstd = sb("rstd", [P, NT], F32)
        shift = sb("shift", [P, NT], F32)
        xT_hi = sb("xT_hi", [P, KC, T], F32R)
        xT_lo = sb("xT_lo", [P, KC, T], F32R)
        router = sb("router", [E, D], F32)
        rT = sb("rT", [P, KC, 2, E], F32R)
        low_logits = sb("low_logits", [P, E, NT], F32)
        logits = sb("logits", [P, E, NT], F32)
        top = sb("top", [P, NT], F32)
        is_top = sb("is_top", [P, E, NT], F32)
        cand = sb("cand", [P, E, NT], F32)
        first = sb("first", [P, NT], F32)
        chosen = sb("chosen", [P, E, NT], BF16)
        upto = sb("upto", [P, E, NT], F32)
        pos = sb("pos", [P, E, NT], F32)
        over = sb("over", [P, E, STEPS], F32)
        tiles_of = sb("tiles_of", [P, E], F32)
        tiles_one = sb("tiles_one", [P, E], F32)
        tiles_upto = sb("tiles_upto", [P, E], F32)
        base = sb("base", [P, E], F32)
        slot = sb("slot", [P, NT], F32)
        slot_row = sb("slot_row", [P, NT], I32)
        plan = sb("plan", [1, 2 * E + 1], I32)
        gexp = sb("gexp", [P, NT], F32)
        gone = sb("gone", [P, NT], F32)
        gate = sb("gate", [P, NT], F32)
        wqkv = sb("wqkv", [P, KC, 3 * D], F32)
        wqkv_hi = sb("wqkv_hi", [P, KC, 3 * D], F32R)
        wqkv_lo = sb("wqkv_lo", [P, KC, 3 * D], F32R)
        wout = sb("wout", [P, KC, D], F32)
        dec_in = sb("dec_in", [HEADS, 1], F32)
        dec_e = sb("dec_e", [HEADS, 1], F32)
        dec_1 = sb("dec_1", [HEADS, 1], F32)
        dec_h = sb("dec_h", [HEADS, 1], F32)
        decay = sb("decay", [P, KC], F32)
        ez = sb("ez", [P, 2, 512], F32)
        rz = sb("rz", [P, 2, 512], F32)
        k_sb = sb("k_sb", [P, 512], F32)
        kv_sb = sb("kv_sb", [P, 512], F32)
        q_sb = sb("q_sb", [P, KC, T], F32)
        ksum = sb("ksum", [P, KC, T], F32)
        kvsum = sb("kvsum", [P, KC, T], F32)
        den = sb("den", [P, NT * HEADS], F32)
        rden = sb("rden", [P, NT * HEADS], F32)
        rdT = sb("rdT", [NT * HEADS, P], F32)
        att_hi = sb("att_hi", [P, KC, T], F32R)
        att_lo = sb("att_lo", [P, KC, T], F32R)
        sgu = sb("sgu", [P, KC, F2], F32)
        sgu_hi = sb("sgu_hi", [P, KC, F2], F32R)
        sgu_lo = sb("sgu_lo", [P, KC, F2], F32R)
        sdn = sb("sdn", [P, FC, D], F32)
        hT_hi = [sb(f"hT_hi{n}", [P, FC, 512], F32R) for n in range(NH)]
        hT_lo = [sb(f"hT_lo{n}", [P, FC, 512], F32R) for n in range(NH)]
        gu = [sb(f"gu{p}", [P, KC, F2], F32) for p in range(2)]
        dn = [sb(f"dn{p}", [P, FC, D], F32) for p in range(2)]
        yT = sb("yT", [P, KC, SLOTS], F32)
        yrow = sb("yrow", [HS, 2, D], F32)

        early = wqkv[:, :, :].rearrange("p c n -> p (c n)")
        xg = early[0:HS, 0:2 * D].rearrange("p (j d) -> p j d", j=2)
        xgT = k_sb[:, 0:KC * SLOTS].rearrange("p (c s) -> p c s", c=KC)
        hr = early[:, 2 * D:2 * D + FC * SLOTS].rearrange("p (f s) -> p f s", f=FC)
        second_hi = wqkv_hi[:, :, :].rearrange("p c n -> p (c n)")
        second_lo = wqkv_lo[:, :, :].rearrange("p c n -> p (c n)")
        sdn_hi = second_hi[:, 0:FC * D].rearrange("p (f d) -> p f d", f=FC)
        sdn_lo = second_lo[:, 0:FC * D].rearrange("p (f d) -> p f d", f=FC)
        wout_hi = second_hi[:, FC * D:(FC + KC) * D].rearrange("p (c d) -> p c d", c=KC)
        wout_lo = second_lo[:, FC * D:(FC + KC) * D].rearrange("p (c d) -> p c d", c=KC)
        h_sb = sgu[:, 0, :].rearrange("p (b t) -> p b t", b=2)
        act_sb = rz
        rspread = ksum
        y_tok = q_sb[:, :, :].rearrange("p c (j d) -> p (c j) d", d=D)

        ps = ctx.enter_context(nc.psum_tensor("ps", [P, 8, 512], F32))
        ROUTE = 6
        logit_ps = ps[:, ROUTE, 0:NT * 2 * E].rearrange("p (i h e) -> p h e i", h=2, e=E)
        rank_ps = ps[:, ROUTE, 128:128 + NT * E]
        count_ps = ps[:, ROUTE, 192:192 + NT * E]

        s_x = [sem(f"s_x{n}") for n in range(NH)]
        s_router = sem("s_router")
        s_dec = sem("s_dec")
        s_wqkv = sem("s_wqkv")
        s_wout = sem("s_wout")
        s_sgu = sem("s_sgu")
        s_sdn = sem("s_sdn")
        s_gu = [sem(f"s_gu{p}") for p in range(2)]
        s_dn = [sem(f"s_dn{p}") for p in range(2)]
        s_zero = sem("s_zero")
        s_const = sem("s_const")
        s_ve = sem("s_ve")
        s_sd = sem("s_sd")
        s_rstd = sem("s_rstd")
        s_xn = sem("s_xn")
        s_xna = sem("s_xna")
        s_xT = sem("s_xT")
        s_rT = sem("s_rT")
        s_rhi = sem("s_rhi")
        s_rlo = sem("s_rlo")
        s_xhi = sem("s_xhi")
        s_xlo = sem("s_xlo")
        s_logit = sem("s_logit")
        s_top = sem("s_top")
        s_gexp = sem("s_gexp")
        s_chosen = sem("s_chosen")
        s_rank = sem("s_rank")
        s_slot = sem("s_slot")
        s_plan = sem("s_plan")
        s_xs = sem("s_xs")
        s_scatter = sem("s_scatter")
        s_whi = sem("s_whi")
        s_wlo = sem("s_wlo")
        s_dece = sem("s_dece")
        s_dech = sem("s_dech")
        s_decp = sem("s_decp")
        s_qkv = sem("s_qkv")
        s_er = sem("s_er")
        s_kv = sem("s_kv")
        s_q = sem("s_q")
        s_qk = sem("s_qk")
        s_den = sem("s_den")
        s_rden = sem("s_rden")
        s_rdT = sem("s_rdT")
        s_rdTc = sem("s_rdTc")
        s_rdram = sem("s_rdram")
        s_spread = sem("s_spread")
        s_att = sem("s_att")
        s_atth = sem("s_atth")
        s_attl = sem("s_attl")
        s_shi = sem("s_shi")
        s_slo = sem("s_slo")
        s_phi = sem("s_phi")
        s_plo = sem("s_plo")
        s_sg = sem("s_sg")
        s_ss = sem("s_ss")
        s_sh = sem("s_sh")
        s_shh = sem("s_shh")
        s_shl = sem("s_shl")
        s_xg = sem("s_xg")
        s_xgT = sem("s_xgT")
        s_xgc = sem("s_xgc")
        s_gup = sem("s_gup")
        s_silu = sem("s_silu")
        s_hr = sem("s_hr")
        s_down = sem("s_down")
        s_yT = sem("s_yT")
        s_yback = sem("s_yback")
        s_yrow = sem("s_yrow")
        s_ystore = sem("s_ystore")
        s_stored = sem("s_stored")
        s_gather = sem("s_gather")
        s_acc = sem("s_acc")
        s_sum = sem("s_sum")
        s_fin = sem("s_fin")
        s_out = sem("s_out")
        s_dve = sem("s_dve")

        block = ctx.enter_context(nc.Block())

        gu_dram = w_gate_up.rearrange("e (c p) n -> e p c n", p=P)
        dn_dram = w_down.rearrange("e (c p) n -> e p c n", p=P)

        def three(o, w_hi, w_lo, m_hi, m_lo, start, stop):
            nc.tensor.matmul(o, w_hi, m_hi, start=start, stop=False)
            nc.tensor.matmul(o, w_hi, m_lo, start=False, stop=False)
            return nc.tensor.matmul(o, w_lo, m_hi, start=False, stop=stop)

        @block.sync
        def _(sp):
            for n in range(NH):
                sp.dma_start(x_sb[:, n * TH:(n + 1) * TH, :], x_rows[:, n * TH:(n + 1) * TH, :]).then_inc(s_x[n], 16)
            sp.dma_start(router[:, :], router_w).then_inc(s_router, 16)
            sp.dma_start(dec_in[:, :], decay_param.rearrange("(h o) -> h o", o=1)).then_inc(s_dec, 16)
            sp.dma_start(wqkv[:, :, :], w_qkv.rearrange("(c p) n -> p c n", p=P)).then_inc(s_wqkv, 16)
            sp.wait_ge(s_wqkv, 16)
            sp.dma_start(sgu[:, :, :], shared_gate_up.rearrange("(c p) n -> p c n", p=P)).then_inc(s_sgu, 16)
            sp.wait_ge(s_const, 1)
            sp.dma_start(sorted_rows.rearrange("r d -> (r d)").rearrange("(p k w) -> p k w", p=P, k=ZK),
                         zeros[:, :].unsqueeze(1).broadcast_to([P, ZK, ZW])).then_inc(s_zero, 16)
            sp.dma_start(sdn[:, :, :], shared_down.rearrange("(c p) n -> p c n", p=P)).then_inc(s_sdn, 16)
            sp.dma_start(wout[:, :, :], w_out.rearrange("(c p) n -> p c n", p=P)).then_inc(s_wout, 16)
            for e in range(2):
                sp.dma_start(gu[e][:, :, :], gu_dram[e]).then_inc(s_gu[e], 16)
                sp.dma_start(dn[e][:, :, :], dn_dram[e]).then_inc(s_dn[e], 16)
            sp.wait_ge(s_rdTc, 1)
            sp.dma_start(rden_rows, rdT[:, :]).then_inc(s_rdram, 16)
            sp.wait_ge(s_rdram, 16)
            for h in range(HEADS):
                c, at = h // HC, (h % HC) * HD
                sp.dma_start(rspread[at:at + HD, c, :].rearrange("p (i t) -> p i t", i=NT),
                             rden_rows.rearrange("(i h) t -> h i t", h=HEADS)[h].unsqueeze(0).broadcast_to([HD, NT, P])).then_inc(s_spread, 16)
            with sp.Fori(0, E // 2 - 1) as i:
                for p in range(2):
                    done = sp.value_load(plan[0:1, bass.ds(2 * i + (E + p + 1), 1)], min_val=1, max_val=TILES)
                    sp.wait_ge(s_gup, 2 * done)
                    sp.dma_start(gu[p][:, :, :], gu_dram[bass.ds(2 * i + (p + 2), 1)].rearrange("e p c n -> p (e c) n")).then_inc(s_gu[p], 16)
                    sp.wait_ge(s_down, done)
                    sp.dma_start(dn[p][:, :, :], dn_dram[bass.ds(2 * i + (p + 2), 1)].rearrange("e p c n -> p (e c) n")).then_inc(s_dn[p], 16)
            for i in range(NT):
                sp.wait_ge(s_fin, i + 1)
                sp.dma_start(out_rows[:, i, :], x_sb[:, i, :]).then_inc(s_out, 16)
            sp.wait_ge(s_out, 16 * NT)

        @block.gpsimd
        def _(pool):
            pool.memset(zeros[:, :], 0.0).then_inc(s_const, 1)
            pool.memset(ident[:, :], 0.0).then_inc(s_const, 1)
            pool.memset(ones[:, :], 1.0).then_inc(s_const, 1)
            pool.memset(head_of[:, :], 1.0).then_inc(s_const, 1)
            pool.memset(spread[:, :, :], 1.0).then_inc(s_const, 1)
            pool.wait_ge(s_const, 5)
            pool.affine_select(out=ident[:, :], in_=ident[:, :], compare_op=ALU.not_equal, fill=1.0,
                               base=0, pattern=[[-1, P]], channel_multiplier=1).then_inc(s_const, 1)
            pool.affine_select(out=before[:, :], in_=ones[:, :], compare_op=ALU.is_gt, fill=0.0,
                               base=0, pattern=[[1, P]], channel_multiplier=-1).then_inc(s_const, 1)
            pool.affine_select(out=head_of[:, :], in_=head_of[:, :], compare_op=ALU.is_ge, fill=0.0,
                               base=0, pattern=[[-HD, HC]], channel_multiplier=1).then_inc(s_const, 1)
            pool.affine_select(out=spread[:, :, :], in_=spread[:, :, :], compare_op=ALU.is_ge, fill=0.0,
                               base=0, pattern=[[P, KC], [1, P]], channel_multiplier=-HD).then_inc(s_const, 1)
            pool.wait_ge(s_const, 9)
            pool.affine_select(out=head_of[:, :], in_=head_of[:, :], compare_op=ALU.is_ge, fill=0.0,
                               base=HD - 1, pattern=[[HD, HC]], channel_multiplier=-1).then_inc(s_const, 1)
            pool.affine_select(out=spread[:, :, :], in_=spread[:, :, :], compare_op=ALU.is_ge, fill=0.0,
                               base=HD - 1, pattern=[[-P, KC], [-1, P]], channel_multiplier=HD).then_inc(s_const, 1)
            pool.iota(em_int[:, :], pattern=[[1, E]], base=-E, channel_multiplier=0).then_inc(s_const, 1)
            pool.iota(steps_int[:, :, :], pattern=[[0, E], [SLOTS, STEPS]], base=SLOTS,
                      channel_multiplier=0).then_inc(s_const, 1)
            pool.memset(restart[:, :, :], 1.0).then_inc(s_const, 1)
            pool.memset(ones8[:, :], 1.0).then_inc(s_const, 1)
            pool.memset(yT[:, :, :], 0.0).then_inc(s_yT, 1)
            pool.memset(yrow[:, :, :], 0.0).then_inc(s_yrow, 1)
            pool.wait_ge(s_const, 15)
            pool.memset(restart[:, :, 0:1], 0.0).then_inc(s_const, 1)
            pool.tensor_copy(em[:, :], em_int[:, :]).then_inc(s_const, 1)
            pool.tensor_copy(steps[:, :, :], steps_int[:, :, :]).then_inc(s_const, 1)
            for k, j in enumerate((1, 2, 0)):
                pool.wait_ge(s_whi, k + 1)
                cols = slice(j * D, (j + 1) * D)
                pool.tensor_tensor(wqkv_lo[:, :, cols], wqkv[:, :, cols], wqkv_hi[:, :, cols].bitcast(F32), ALU.subtract).then_inc(s_wlo, 1)
            for k in range(4):
                pool.wait_ge(s_shi, k + 1)
                c, cols = k // 2, slice((k % 2) * F, (k % 2 + 1) * F)
                pool.tensor_tensor(sgu_lo[:, c, cols], sgu[:, c, cols], sgu_hi[:, c, cols].bitcast(F32), ALU.subtract).then_inc(s_slo, 1)
            pool.wait_ge(s_zero, 16)
            pool.wait_ge(s_yrow, 1)
            pool.dma_start(sorted_rows[0:SLOTS, :].rearrange("(j p) d -> p j d", p=HS), yrow[:, :, :]).then_inc(s_ystore, 16)

            pool.wait_ge(s_xT, NT)
            pool.wait_ge(s_slot, 1)
            for i in range(NT):
                pool.tensor_scalar(xn[:, i, :], xn[:, i, :], gate[:, i:i + 1], None, ALU.mult).then_inc(s_xs, 1)
            pool.wait_ge(s_ystore, 16)
            for i in range(NT):
                pool.wait_ge(s_xs, i + 1)
                pool.indirect_dma_start(sorted_rows, bass.IndirectOffsetOnAxis(ap=slot_row[:, i:i + 1], axis=0),
                                        xn[:, i, :], None).then_inc(s_scatter, 16)
            pool.wait_ge(s_scatter, 16 * NT)
            pool.wait_ge(s_slo, 4)
            pool.dma_start(xg, sorted_rows[SLOTS:2 * SLOTS, :].rearrange("(j p) d -> p j d", p=HS)).then_inc(s_xg, 16)
            pool.wait_ge(s_plan, 3)
            total = pool.value_load(plan[0:1, 2 * E:2 * E + 1], min_val=E, max_val=TILES)
            with pool.Fori(0, total) as t:
                pool.wait_ge(s_xgT, t + 1)
                pool.dma_start(xg, sorted_rows[bass.ds(t * SLOTS + 2 * SLOTS, SLOTS), :].rearrange("(j p) d -> p j d", p=HS)).then_inc(s_xg, 16)
                pool.wait_ge(s_yrow, t + 2)
                pool.dma_start(sorted_rows[bass.ds(t * SLOTS, SLOTS), :].rearrange("(j p) d -> p j d", p=HS), yrow[:, :, :]).then_inc(s_ystore, 16)
            pool.wait_ge(s_yrow, total + 2)
            pool.dma_start(sorted_rows[bass.ds(total * SLOTS, SLOTS), :].rearrange("(j p) d -> p j d", p=HS), yrow[:, :, :]).then_inc(s_ystore, 16)
            pool.wait_ge(s_ystore, 16 * total + 32)
            pool.sem_inc(s_stored, 1)
            pool.wait_ge(s_stored, 1)
            for i in range(NT):
                pool.indirect_dma_start(y_tok[:, i, :], None, sorted_rows,
                                        bass.IndirectOffsetOnAxis(ap=slot_row[:, i:i + 1], axis=0)).then_inc(s_gather, 16)
            pool.wait_ge(s_gather, 16 * NT)
            pool.wait_ge(s_xg, 16 * total + 16)

        @block.scalar
        def _(act):
            A = nc.scalar.activation

            def norm(n):
                act.wait_ge(s_rstd, n + 1)
                for i in (n * TH + 2, n * TH + 3):
                    A(xn[:, i, :], x_sb[:, i, :], ACT.Identity, scale=rstd[:, i:i + 1], bias=shift[:, i:i + 1]).then_inc(s_xna, 1)

            def x_hi(n):
                act.wait_ge(s_xT, TH * (n + 1))
                for c in range(KC):
                    A(xT_hi[:, c, n * 512:(n + 1) * 512], ps[:, 4 + c, :], ACT.Copy).then_inc(s_xhi, 1)

            def w_hi(j):
                A(wqkv_hi[:, :, j * D:(j + 1) * D], wqkv[:, :, j * D:(j + 1) * D], ACT.Copy).then_inc(s_whi, 1)

            act.wait_ge(s_ve, 1)
            A(sd[:, 0:TH], ve[:, 0:TH], ACT.Sqrt).then_inc(s_sd, 1)
            norm(0)
            act.wait_ge(s_rT, 1)
            A(rT[:, :, 0, :], ps[:, 7, 0:KC * E].rearrange("p (c e) -> p c e", e=E), ACT.Copy).then_inc(s_rhi, 1)
            act.wait_ge(s_wqkv, 16)
            w_hi(1)
            x_hi(0)
            w_hi(2)
            w_hi(0)
            act.wait_ge(s_ve, 2)
            A(sd[:, TH:NT], ve[:, TH:NT], ACT.Sqrt).then_inc(s_sd, 1)
            norm(1)
            act.wait_ge(s_dec, 16)
            A(dec_e[:, :], dec_in[:, :], ACT.Exp, scale=-1.0).then_inc(s_dece, 1)
            for a in range(2 * NH):
                if a == 1:
                    x_hi(1)
                if a == 2:
                    act.wait_ge(s_top, 1)
                    A(gexp[:, :], top[:, :], ACT.Exp, scale=-1.0).then_inc(s_gexp, 1)
                for j, t in ((0, 3 * a), (1, 3 * a + 2)):
                    act.wait_ge(s_qkv, t + 1)
                    if a >= 1:
                        act.wait_ge((s_kv, s_q)[j], a)
                    A(ez[:, j, :], ps[:, t % 4, :], ACT.Exp)
                    A(rz[:, j, :], ps[:, t % 4, :], ACT.Relu).then_inc(s_er, 1)
                if a < 2:
                    act.wait_ge(s_sgu, 16)
                    for h in range(2):
                        A(sgu_hi[:, a, h * F:(h + 1) * F], sgu[:, a, h * F:(h + 1) * F], ACT.Copy).then_inc(s_shi, 1)

            def shared_silu(n):
                for f in range(FC + 1):
                    k = n * FC + f
                    if f < FC:
                        act.wait_ge(s_sg, 2 * k + 1)
                        if k >= 2:
                            act.wait_ge(s_sh, k - 1)
                        A(act_sb[:, k % 2, :], ps[:, 2 * (k % 2), :], ACT.Silu).then_inc(s_ss, 1)
                    if f >= 1:
                        act.wait_ge(s_sh, k)
                        A(hT_hi[n][:, f - 1, :], h_sb[:, (k - 1) % 2, :], ACT.Copy).then_inc(s_shh, 1)

            act.wait_ge(s_q, 2 * NH)
            shared_silu(0)
            act.wait_ge(s_sdn, 16)
            A(sdn_hi, sdn[:, :, :], ACT.Copy).then_inc(s_phi, 1)
            act.wait_ge(s_wout, 16)
            A(wout_hi, wout[:, :, :], ACT.Copy).then_inc(s_phi, 1)
            act.wait_ge(s_rdT, 1)
            A(rdT[:, :], ps[:, 7, 0:P], ACT.Copy).then_inc(s_rdTc, 1)

            def sorted_copy(done):
                act.wait_ge(s_xgT, done)
                A(xgT, ps[:, 4, 0:KC * SLOTS].rearrange("p (c s) -> p c s", c=KC), ACT.Copy).then_inc(s_xgc, 1)

            sorted_copy(1)
            act.wait_ge(s_plan, 3)
            total = act.value_load(plan[0:1, 2 * E:2 * E + 1], min_val=E, max_val=TILES)
            with act.Fori(0, total) as t:
                for h in range(2):
                    act.wait_ge(s_gup, 2 * t + (h + 1))
                    A(act_sb[:, h, 0:2 * SLOTS], ps[:, 2 * h, 0:2 * SLOTS], ACT.Silu).then_inc(s_silu, 1)
                sorted_copy(t + 2)
                act.wait_ge(s_down, t + 1)
                A(yT[:, :, :], ps[:, 5:7, 0:SLOTS], ACT.Copy).then_inc(s_yT, 1)
            for c in range(KC):
                act.wait_ge(s_att, c + 1)
                A(att_hi[:, c, :], kvsum[:, c, :], ACT.Copy).then_inc(s_atth, 1)
            shared_silu(1)

        @block.vector
        def _(dve):
            steps_done = [0]

            def link(ins):
                steps_done[0] += 1
                ins.then_inc(s_dve, 1)
                dve.wait_ge(s_dve, steps_done[0])

            V = nc.vector

            def layer_norm(n):
                dve.wait_ge(s_x[n], 16)
                h = slice(n * TH, (n + 1) * TH)
                for i in range(n * TH, (n + 1) * TH):
                    ins = V.bn_stats(bn[:, i, :], x_sb[:, i, :])
                link(ins)
                for i in range(n * TH, (n + 1) * TH):
                    ins = V.bn_aggr(mv[:, i, :], bn[:, i, :])
                link(ins)
                V.tensor_scalar(ve[:, h], mv[:, h, 1], EPS_LN, None, ALU.add).then_inc(s_ve, 1)
                dve.wait_ge(s_sd, n + 1)
                link(V.reciprocal(rs[:, h], sd[:, h]))
                link(V.tensor_tensor(rt[:, h], rs[:, h], rs[:, h], ALU.mult))
                link(V.tensor_tensor(rt[:, h], rt[:, h], ve[:, h], ALU.mult))
                link(V.tensor_scalar(rt[:, h], rt[:, h], -0.5, 1.5, ALU.mult, ALU.add))
                link(V.tensor_tensor(rstd[:, h], rs[:, h], rt[:, h], ALU.mult))
                V.scalar_tensor_tensor(shift[:, h], mv[:, h, 0], -1.0, rstd[:, h], ALU.mult, ALU.mult).then_inc(s_rstd, 1)
                for i in (n * TH, n * TH + 1):
                    V.tensor_scalar(xn[:, i, :], x_sb[:, i, :], mv[:, i, 0:1], rstd[:, i:i + 1], ALU.subtract, ALU.mult).then_inc(s_xn, 1)

            def x_lo(n):
                for c in range(KC):
                    dve.wait_ge(s_xhi, 2 * n + c + 1)
                    cols = slice(n * 512, (n + 1) * 512)
                    V.tensor_tensor(xT_lo[:, c, cols], ps[:, 4 + c, :], xT_hi[:, c, cols].bitcast(F32), ALU.subtract).then_inc(s_xlo, 1)

            em_b = em[:, :].unsqueeze(2).broadcast_to([P, E, NT])
            flat = "p e i -> p (e i)"

            def choose():
                dve.wait_ge(s_logit, 1)
                link(V.tensor_copy(low_logits[:, :, :], logit_ps[:, 1, :, :]))
                link(V.tensor_tensor(logits[:, :, :], low_logits[:, :, :], logit_ps[:, 0, :, :], ALU.add))
                V.tensor_reduce(top[:, :], logits[:, :, :].rearrange("p e i -> p i e"), AX.X, ALU.max).then_inc(s_top, 1)
                dve.wait_ge(s_top, 1)
                link(V.tensor_tensor(is_top[:, :, :], logits[:, :, :], top[:, :].unsqueeze(1).broadcast_to([P, E, NT]), ALU.is_equal))
                dve.wait_ge(s_const, 18)
                link(V.tensor_tensor(cand[:, :, :], is_top[:, :, :], em_b, ALU.mult))
                link(V.tensor_reduce(first[:, :], cand[:, :, :].rearrange("p e i -> p i e"), AX.X, ALU.min))
                V.tensor_tensor(chosen[:, :, :], em_b, first[:, :].unsqueeze(1).broadcast_to([P, E, NT]), ALU.is_equal).then_inc(s_chosen, 1)

            def place():
                dve.wait_ge(s_rank, 1)
                link(V.tensor_tensor_scan(upto[:, :, :].rearrange(flat), restart[:, :, :].rearrange(flat), count_ps, 0.0, ALU.mult, ALU.add))
                link(V.tensor_tensor(pos[:, :, :].rearrange(flat), upto[:, :, :].rearrange(flat), count_ps, ALU.subtract))
                link(V.tensor_tensor(pos[:, :, :].rearrange(flat), pos[:, :, :].rearrange(flat), rank_ps, ALU.add))
                link(V.tensor_tensor(over[:, :, :], upto[:, :, NT - 1:NT].broadcast_to([P, E, STEPS]), steps[:, :, :], ALU.is_gt))
                link(V.tensor_reduce(tiles_of[:, :], over[:, :, :], AX.X, ALU.add))
                link(V.tensor_scalar(tiles_one[:, :], tiles_of[:, :], 1.0, None, ALU.add))
                link(V.tensor_tensor_scan(tiles_upto[:, :], ones8[:, :], tiles_one[:, :], 0.0, ALU.mult, ALU.add))
                link(V.tensor_tensor(base[:, :], tiles_upto[:, :], tiles_one[:, :], ALU.subtract))
                link(V.scalar_tensor_tensor(pos[:, :, :], base[:, :].unsqueeze(2).broadcast_to([P, E, NT]), float(SLOTS), pos[:, :, :], ALU.mult, ALU.add))
                link(V.tensor_tensor(pos[:, :, :], pos[:, :, :], chosen[:, :, :], ALU.mult))
                link(V.tensor_reduce(slot[:, :], pos[:, :, :].rearrange("p e i -> p i e"), AX.X, ALU.add))
                dve.wait_ge(s_gexp, 1)
                link(V.tensor_scalar(gone[:, :], gexp[:, :], 1.0, None, ALU.add))
                V.reciprocal(gate[:, :], gone[:, :])
                V.tensor_scalar(slot_row[:, :], slot[:, :], float(SLOTS), None, ALU.add).then_inc(s_slot, 1)
                V.tensor_copy(plan[0:1, 0:E], tiles_one[0:1, :]).then_inc(s_plan, 1)
                V.tensor_copy(plan[0:1, E:2 * E], base[0:1, :]).then_inc(s_plan, 1)
                V.tensor_copy(plan[0:1, 2 * E:2 * E + 1], tiles_upto[0:1, E - 1:E]).then_inc(s_plan, 1)

            layer_norm(0)
            dve.wait_ge(s_rhi, 1)
            V.tensor_tensor(rT[:, :, 1, :], ps[:, 7, 0:KC * E].rearrange("p (c e) -> p c e", e=E),
                            rT[:, :, 0, :].bitcast(F32), ALU.subtract).then_inc(s_rlo, 1)
            x_lo(0)
            layer_norm(1)
            dve.wait_ge(s_dece, 1)
            link(V.tensor_scalar(dec_1[:, :], dec_e[:, :], 1.0, None, ALU.add))
            V.reciprocal(dec_h[:, :], dec_1[:, :]).then_inc(s_dech, 1)
            for a in range(2 * NH):
                if a == 1:
                    x_lo(1)
                if a == 2:
                    choose()
                n, c = a // 2, a % 2
                cols = slice(n * 512, (n + 1) * 512)
                rate = decay[:, c:c + 1].broadcast_to([P, 512])
                dve.wait_ge(s_er, 2 * a + 1)
                link(V.scalar_tensor_tensor(k_sb[:, :], ez[:, 0, :], 1.0, rz[:, 0, :], ALU.min, ALU.add))
                dve.wait_ge(s_qkv, 3 * a + 2)
                V.tensor_tensor(kv_sb[:, :], k_sb[:, :], ps[:, (3 * a + 1) % 4, :], ALU.mult).then_inc(s_kv, 1)
                if a == 0:
                    dve.wait_ge(s_decp, 1)
                    link(V.tensor_copy(decay[:, :], ps[:, 7, 64:64 + KC]))
                V.tensor_tensor_scan(ksum[:, c, cols], rate, k_sb[:, :], ksum[:, c, n * 512 - 1:n * 512] if n else 0.0, ALU.mult, ALU.add)
                dve.wait_ge(s_kv, a + 1)
                link(V.tensor_tensor_scan(kvsum[:, c, cols], rate, kv_sb[:, :], kvsum[:, c, n * 512 - 1:n * 512] if n else 0.0, ALU.mult, ALU.add))
                dve.wait_ge(s_er, 2 * a + 2)
                V.scalar_tensor_tensor(q_sb[:, c, cols], ez[:, 1, :], 1.0, rz[:, 1, :], ALU.min, ALU.add).then_inc(s_q, 1)
                if a == 2:
                    place()
            dve.wait_ge(s_q, 2 * NH)
            for c in range(KC):
                V.tensor_tensor(ksum[:, c, :], q_sb[:, c, :], ksum[:, c, :], ALU.mult).then_inc(s_qk, 1)

            def shared_hidden(n, f):
                k = n * FC + f
                if f < FC:
                    dve.wait_ge(s_ss, k + 1)
                    dve.wait_ge(s_sg, 2 * k + 2)
                    if k >= 2:
                        dve.wait_ge(s_shl, k - 1)
                    V.tensor_tensor(h_sb[:, k % 2, :], act_sb[:, k % 2, :], ps[:, 2 * (k % 2) + 1, :], ALU.mult).then_inc(s_sh, 1)
                if f >= 1:
                    dve.wait_ge(s_shh, k)
                    V.tensor_tensor(hT_lo[n][:, f - 1, :], h_sb[:, (k - 1) % 2, :], hT_hi[n][:, f - 1, :].bitcast(F32), ALU.subtract).then_inc(s_shl, 1)

            dve.wait_ge(s_slo, 4)
            shared_hidden(0, 0)
            for f in range(1, FC):
                shared_hidden(0, f)
                if f <= KC:
                    link(V.tensor_tensor(kvsum[:, f - 1, :], q_sb[:, f - 1, :], kvsum[:, f - 1, :], ALU.mult))
            dve.wait_ge(s_den, 1)
            link(V.tensor_scalar(den[:, :], ps[:, ROUTE, 0:NT * HEADS], EPS_DEN, None, ALU.max))
            V.reciprocal(rden[:, :], den[:, :]).then_inc(s_rden, 1)
            shared_hidden(0, FC)
            dve.wait_ge(s_phi, 2)
            V.tensor_tensor(sdn_lo, sdn[:, :, :], sdn_hi.bitcast(F32), ALU.subtract).then_inc(s_plo, 1)
            V.tensor_tensor(wout_lo, wout[:, :, :], wout_hi.bitcast(F32), ALU.subtract).then_inc(s_plo, 1)

            def rows_copy(t):
                dve.wait_ge(s_yback, t + 1)
                dve.wait_ge(s_ystore, 16 * t + 16)
                V.tensor_copy(yrow[:, :, :].rearrange("p j d -> p (j d)"), ps[0:HS, 7, :]).then_inc(s_yrow, 1)

            dve.wait_ge(s_plan, 3)
            total = dve.value_load(plan[0:1, 2 * E:2 * E + 1], min_val=E, max_val=TILES)
            with dve.Fori(0, total) as t:
                for h in range(2):
                    dve.wait_ge(s_silu, 2 * t + (h + 1))
                    V.tensor_tensor(hr[:, 2 * h:2 * h + 2, :].rearrange("p f s -> p (f s)"), act_sb[:, h, 0:2 * SLOTS],
                                    ps[:, 2 * h + 1, 0:2 * SLOTS], ALU.mult).then_inc(s_hr, 1)
                    if h == 0:
                        rows_copy(t)
            rows_copy(total)
            dve.wait_ge(s_spread, 16 * HEADS)
            for c in range(KC):
                V.tensor_tensor(kvsum[:, c, :], kvsum[:, c, :], rspread[:, c, :], ALU.mult).then_inc(s_att, 1)
            for f in range(FC + 1):
                shared_hidden(1, f)
                if f < KC:
                    dve.wait_ge(s_atth, f + 1)
                    V.tensor_tensor(att_lo[:, f, :], kvsum[:, f, :], att_hi[:, f, :].bitcast(F32), ALU.subtract).then_inc(s_attl, 1)
            dve.wait_ge(s_gather, 16 * NT)
            for i in range(NT):
                V.tensor_tensor(x_sb[:, i, :], x_sb[:, i, :], y_tok[:, i, :], ALU.add).then_inc(s_sum, 1)
            for i in range(NT):
                dve.wait_ge(s_acc, i + 1)
                dve.wait_ge(s_sum, i + 1)
                V.tensor_tensor(x_sb[:, i, :], x_sb[:, i, :], ps[:, 4 + i % TH, 0:D], ALU.add).then_inc(s_fin, 1)

        @block.tensor
        def _(pe):
            mm = nc.tensor.matmul
            tr = nc.tensor.transpose

            def transpose_tokens(n):
                for j in range(TH):
                    i = n * TH + j
                    if j < 2:
                        pe.wait_ge(s_xn, 2 * n + j + 1)
                    else:
                        pe.wait_ge(s_xna, 2 * n + j - 1)
                    if n and j == 0:
                        pe.wait_ge(s_xlo, 2)
                    for c in range(KC):
                        ins = tr(ps[:, 4 + c, j * P:(j + 1) * P], xn[:, i, c * P:(c + 1) * P], ident[:, :])
                    ins.then_inc(s_xT, 1)

            def router_logits():
                pe.wait_ge(s_rlo, 1)
                pe.wait_ge(s_xlo, 4)
                for i in range(NT):
                    cols = slice(i * P, (i + 1) * P)
                    both = ps[:, ROUTE, i * 2 * E:(i + 1) * 2 * E]
                    mm(both, xT_hi[:, 0, cols], rT[:, 0, :, :].rearrange("p h e -> p (h e)"), start=True, stop=False)
                    for c in range(KC):
                        mm(both[:, 0:E], xT_lo[:, c, cols], rT[:, c, 0, :], start=False, stop=False, skip_group_check=True)
                    ins = mm(both, xT_hi[:, 1, cols], rT[:, 1, :, :].rearrange("p h e -> p (h e)"), start=False, stop=True)
                ins.then_inc(s_logit, 1)

            def ranks():
                pe.wait_ge(s_chosen, 1)
                pick = chosen[:, :, :].rearrange("p e i -> p (e i)")
                mm(rank_ps, before[:, :], pick, start=True, stop=True)
                mm(count_ps, ones[:, :], pick, start=True, stop=True).then_inc(s_rank, 1)

            def qkv_tile(t):
                a, j = t // 3, (1, 2, 0)[t % 3]
                n, c = a // 2, a % 2
                pe.wait_ge(s_wlo, min(t + 1, 3))
                pe.wait_ge(s_xlo, 2 * n + 2)
                if t >= 4:
                    u = t - 4
                    if u % 3 == 1:
                        pe.wait_ge(s_kv, u // 3 + 1)
                    else:
                        pe.wait_ge(s_er, 2 * (u // 3) + (1 if u % 3 == 0 else 2))
                for kc in range(KC):
                    col = j * D + c * P
                    ins = three(ps[:, t % 4, :], wqkv_hi[:, kc, col:col + P], wqkv_lo[:, kc, col:col + P],
                                xT_hi[:, kc, n * 512:(n + 1) * 512], xT_lo[:, kc, n * 512:(n + 1) * 512], kc == 0, kc == KC - 1)
                ins.then_inc(s_qkv, 1)

            def shared_gate_up_tiles(n, fs):
                for f in fs:
                    k = n * FC + f
                    for u in range(2):
                        if k == 0 and u == 0:
                            pe.wait_ge(s_er, 4 * NH)
                            pe.wait_ge(s_kv, 2 * NH)
                            pe.wait_ge(s_slo, 4)
                        if k >= 2:
                            pe.wait_ge((s_ss, s_sh)[u], k - 1)
                        for kc in range(KC):
                            col = u * F + f * P
                            ins = three(ps[:, 2 * (k % 2) + u, :], sgu_hi[:, kc, col:col + P], sgu_lo[:, kc, col:col + P],
                                        xT_hi[:, kc, n * 512:(n + 1) * 512], xT_lo[:, kc, n * 512:(n + 1) * 512], kc == 0, kc == KC - 1)
                        ins.then_inc(s_sg, 1)

            def transpose_sorted(loaded):
                pe.wait_ge(s_xg, loaded)
                for c in range(KC):
                    for j in range(2):
                        col = c * SLOTS + j * HS
                        ins = tr(ps[:, 4, col:col + HS], xg[:, j, c * P:(c + 1) * P], ident[0:HS, 0:HS])
                ins.then_inc(s_xgT, 1)

            def transpose_back(copied):
                pe.wait_ge(s_yT, copied)
                for c in range(KC):
                    for j in range(2):
                        ins = tr(ps[0:HS, 7, j * D + c * P:j * D + (c + 1) * P], yT[:, c, j * HS:(j + 1) * HS], ident[:, :])
                ins.then_inc(s_yback, 1)

            pe.wait_ge(s_const, 11)
            pe.wait_ge(s_router, 16)
            for c in range(KC):
                ins = tr(ps[:, 7, c * E:(c + 1) * E], router[:, c * P:(c + 1) * P], ident[0:E, 0:E])
            ins.then_inc(s_rT, 1)
            transpose_tokens(0)
            for t in range(3):
                qkv_tile(t)
            transpose_tokens(1)
            pe.wait_ge(s_dech, 1)
            for c in range(KC):
                ins = mm(ps[:, 7, 64 + c:65 + c], spread[:, c, :], dec_h[:, :], start=True, stop=True)
            ins.then_inc(s_decp, 1)
            for t in range(3, 6):
                qkv_tile(t)
            router_logits()
            for t in range(6, 9):
                qkv_tile(t)
            ranks()
            for t in range(9, 12):
                qkv_tile(t)
            shared_gate_up_tiles(0, range(3))
            pe.wait_ge(s_qk, KC)
            for i in range(NT):
                for c in range(KC):
                    col = i * HEADS + c * HC
                    ins = mm(ps[:, ROUTE, col:col + HC], ksum[:, c, i * P:(i + 1) * P], head_of[:, :], start=True, stop=True)
            ins.then_inc(s_den, 1)
            shared_gate_up_tiles(0, range(3, FC))
            pe.wait_ge(s_rden, 1)
            tr(ps[:, 7, 0:P], rden[:, :], ident[:, :]).then_inc(s_rdT, 1)
            transpose_sorted(16)
            pe.wait_ge(s_sh, FC)
            pe.wait_ge(s_rdTc, 1)
            pe.wait_ge(s_plan, 3)
            with pe.Fori(0, E // 2) as i:
                for p in range(2):
                    pe.wait_ge(s_gu[p], 16 * i + 16)
                    count = pe.value_load(plan[0:1, bass.ds(2 * i + p, 1)], min_val=1, max_val=TILES)
                    start = pe.value_load(plan[0:1, bass.ds(2 * i + (E + p), 1)], min_val=0, max_val=TILES)
                    with pe.Fori(0, count) as j:
                        t = start + j
                        pe.wait_ge(s_xgc, t + 1)
                        for h in range(2):
                            for u in range(2):
                                for f in (2 * h, 2 * h + 1):
                                    for kc in range(KC):
                                        col = u * F + f * P
                                        ins = mm(ps[:, 2 * h + u, (f % 2) * SLOTS:(f % 2 + 1) * SLOTS],
                                                 gu[p][:, kc, col:col + P], xgT[:, kc, :], start=(kc == 0), stop=(kc == KC - 1))
                            ins.then_inc(s_gup, 1)
                            if h == 0:
                                pe.wait_ge(s_yrow, t + 1)
                                transpose_back(t + 1)
                        transpose_sorted(16 * t + 32)
                        pe.wait_ge(s_dn[p], 16 * i + 16)
                        for h in range(2):
                            pe.wait_ge(s_hr, 2 * t + (h + 1))
                            for c in range(KC):
                                for f in (2 * h, 2 * h + 1):
                                    ins = mm(ps[:, 5 + c, 0:SLOTS], dn[p][:, f, c * P:(c + 1) * P], hr[:, f, :],
                                             start=(f == 0), stop=(f == FC - 1))
                        ins.then_inc(s_down, 1)

            total = pe.value_load(plan[0:1, 2 * E:2 * E + 1], min_val=E, max_val=TILES)
            pe.wait_ge(s_yrow, total + 1)
            transpose_back(total + 1)
            shared_gate_up_tiles(1, range(FC))

            def finish(n):
                for i in range(n * TH, (n + 1) * TH):
                    j = i % TH
                    if n:
                        pe.wait_ge(s_fin, i - TH + 1)
                    rows = slice(j * P, (j + 1) * P)
                    o = ps[:, 4 + j, 0:D]
                    for f in range(FC):
                        three(o, hT_hi[n][:, f, rows], hT_lo[n][:, f, rows], sdn_hi[:, f, :], sdn_lo[:, f, :], f == 0, False)
                    rows = slice(i * P, (i + 1) * P)
                    for c in range(KC):
                        ins = three(o, att_hi[:, c, rows], att_lo[:, c, rows], wout_hi[:, c, :], wout_lo[:, c, :], False, c == KC - 1)
                    ins.then_inc(s_acc, 1)

            pe.wait_ge(s_shl, FC)
            pe.wait_ge(s_plo, 2)
            pe.wait_ge(s_attl, KC)
            pe.wait_ge(s_xgc, total + 1)
            pe.wait_ge(s_yrow, total + 2)
            finish(0)
            pe.wait_ge(s_shl, 2 * FC)
            finish(1)

_INS = ['L0_attn_x', 'L0_attn_w_qkv', 'L0_attn_w_out', 'L0_attn_decay_param', 'L0_ffn_router_w', 'L0_ffn_w_gate_up',
        'L0_ffn_w_down', 'L0_ffn_shared_gate_up', 'L0_ffn_shared_down']
_OUTS = [((1, 1024, 256), 'float32')]


def kernel(**inputs):
    import numpy as _np
    import concourse.bacc as _bacc
    from concourse import mybir as _mybir
    from concourse.bass_utils import run_bass_kernel_spmd as _run

    nc = _bacc.Bacc("TRN2", target_bir_lowering=False, num_devices=1)
    arrays, args = {}, []
    for name in _INS:
        a = _np.ascontiguousarray(inputs[name])
        arrays[f"in_{name}_dram"] = a
        args.append(nc.dram_tensor(f"in_{name}_dram", a.shape, _mybir.dt.from_np(a.dtype), kind="ExternalInput").ap())
    for i, (shape, dtype) in enumerate(_OUTS):
        dt = _mybir.dt.from_np(_np.dtype(dtype))
        args.append(nc.dram_tensor(f"out_{i}_dram", shape, dt, kind="ExternalOutput").ap())
    build(nc, *args)
    r = _run(nc, [arrays], core_ids=[0])
    return r.results[0]["out_0_dram"]
```

```python
from contextlib import ExitStack

import concourse.bass as bass
from concourse import mybir

ALU = mybir.AluOpType
ACT = mybir.ActivationFunctionType
AX = mybir.AxisListType
F32 = mybir.dt.float32
F32R = mybir.dt.float32r
BF16 = mybir.dt.bfloat16
I32 = mybir.dt.int32

P = 128
HEADS = 16
EPS_LN = 1e-5
EPS_DEN = 1e-6
SLOTS = 144
HS = SLOTS // 2
WARM = 14


def build(nc, x, w_qkv, w_out, decay_param, router_w, w_gate_up, w_down, shared_gate_up, shared_down, out):
    _, T, D = x.shape
    E, _, F2 = w_gate_up.shape
    F = F2 // 2
    NT = T // P
    KC = D // P
    FC = F // P
    NH = T // 512
    TH = NT // NH
    HC = HEADS // KC
    HD = D // HEADS
    TILES = (T + E * (SLOTS - 1)) // SLOTS
    STEPS = (T - 1) // SLOTS
    ROWS = (TILES + 2) * SLOTS

    x_rows = x.rearrange("a (i p) d -> p (a i) d", p=P)
    out_rows = out.rearrange("a (i p) d -> p (a i) d", p=P)
    sorted_rows = nc.dram_tensor("sorted_rows", (ROWS, D), F32, kind="Internal").ap()
    rden_rows = nc.dram_tensor("rden_rows", (NT * D, P), F32, kind="Internal").ap()

    with ExitStack() as ctx:
        def sb(name, shape, dt):
            return ctx.enter_context(nc.sbuf_tensor(name, shape, dt))

        def sem(name):
            return ctx.enter_context(nc.semaphore(name))

        ident = sb("ident", [P, P], F32)
        before = sb("before", [P, P], BF16)
        ones = sb("ones", [P, P], BF16)
        head_of = sb("head_of", [P, HC], F32)
        spread = sb("spread", [HEADS, KC, P], F32)
        em = sb("em", [P, E], F32)
        em_int = sb("em_int", [P, E], I32)
        steps_int = sb("steps_int", [P, E, STEPS], I32)
        steps = sb("steps", [P, E, STEPS], F32)
        restart = sb("restart", [P, E, NT], F32)
        ones8 = sb("ones8", [P, E], F32)
        ZK = 16
        ZW = ROWS * D // P // ZK
        zeros = sb("zeros", [P, ZW], F32)
        x_sb = sb("x_sb", [P, NT, D], F32)
        xn = sb("xn", [P, NT, D], F32)
        bn = sb("bn", [P, NT, 6], F32)
        mv = sb("mv", [P, NT, 2], F32)
        ve = sb("ve", [P, NT], F32)
        sd = sb("sd", [P, NT], F32)
        rs = sb("rs", [P, NT], F32)
        rt = sb("rt", [P, NT], F32)
        rstd = sb("rstd", [P, NT], F32)
        shift = sb("shift", [P, NT], F32)
        xT_hi = sb("xT_hi", [P, KC, T], F32R)
        xT_lo = sb("xT_lo", [P, KC, T], F32R)
        router = sb("router", [E, D], F32)
        rT = sb("rT", [P, KC, 2, E], F32R)
        low_logits = sb("low_logits", [P, E, NT], F32)
        logits = sb("logits", [P, E, NT], F32)
        top = sb("top", [P, NT], F32)
        is_top = sb("is_top", [P, E, NT], F32)
        cand = sb("cand", [P, E, NT], F32)
        first = sb("first", [P, NT], F32)
        chosen = sb("chosen", [P, E, NT], BF16)
        upto = sb("upto", [P, E, NT], F32)
        pos = sb("pos", [P, E, NT], F32)
        over = sb("over", [P, E, STEPS], F32)
        tiles_of = sb("tiles_of", [P, E], F32)
        tiles_one = sb("tiles_one", [P, E], F32)
        tiles_upto = sb("tiles_upto", [P, E], F32)
        base = sb("base", [P, E], F32)
        slot = sb("slot", [P, NT], F32)
        slot_row = sb("slot_row", [P, NT], I32)
        plan = sb("plan", [1, E], I32)
        gexp = sb("gexp", [P, NT], F32)
        gone = sb("gone", [P, NT], F32)
        gate = sb("gate", [P, NT], F32)
        wqkv = sb("wqkv", [P, KC, 3 * D], F32)
        wqkv_hi = sb("wqkv_hi", [P, KC, 3 * D], F32R)
        wqkv_lo = sb("wqkv_lo", [P, KC, 3 * D], F32R)
        wout = sb("wout", [P, KC, D], F32)
        dec_in = sb("dec_in", [HEADS, 1], F32)
        dec_e = sb("dec_e", [HEADS, 1], F32)
        dec_1 = sb("dec_1", [HEADS, 1], F32)
        dec_h = sb("dec_h", [HEADS, 1], F32)
        decay = sb("decay", [P, KC], F32)
        ez = sb("ez", [P, 2, 512], F32)
        rz = sb("rz", [P, 2, 512], F32)
        k_sb = sb("k_sb", [P, 512], F32)
        kv_sb = sb("kv_sb", [P, 512], F32)
        q_sb = sb("q_sb", [P, KC, T], F32)
        ksum = sb("ksum", [P, KC, T], F32)
        kvsum = sb("kvsum", [P, KC, T], F32)
        den = sb("den", [P, NT * HEADS], F32)
        rden = sb("rden", [P, NT * HEADS], F32)
        rdT = sb("rdT", [NT * HEADS, P], F32)
        att_hi = sb("att_hi", [P, KC, T], F32R)
        att_lo = sb("att_lo", [P, KC, T], F32R)
        sgu = sb("sgu", [P, KC, F2], F32)
        sgu_hi = sb("sgu_hi", [P, KC, F2], F32R)
        sgu_lo = sb("sgu_lo", [P, KC, F2], F32R)
        sdn = sb("sdn", [P, FC, D], F32)
        hT_hi = [sb(f"hT_hi{n}", [P, FC, 512], F32R) for n in range(NH)]
        hT_lo = [sb(f"hT_lo{n}", [P, FC, 512], F32R) for n in range(NH)]
        gu = [sb(f"gu{p}", [P, KC, F2], F32) for p in range(2)]
        dn = [sb(f"dn{p}", [P, FC, D], F32) for p in range(2)]
        yT = sb("yT", [P, KC, SLOTS], F32)
        yrow = sb("yrow", [HS, 2, D], F32)

        early = wqkv[:, :, :].rearrange("p c n -> p (c n)")
        xg = early[0:HS, 0:2 * D].rearrange("p (j d) -> p j d", j=2)
        xgT = k_sb[:, 0:KC * SLOTS].rearrange("p (c s) -> p c s", c=KC)
        hr = early[:, 2 * D:2 * D + FC * SLOTS].rearrange("p (f s) -> p f s", f=FC)
        second_hi = wqkv_hi[:, :, :].rearrange("p c n -> p (c n)")
        second_lo = wqkv_lo[:, :, :].rearrange("p c n -> p (c n)")
        sdn_hi = second_hi[:, 0:FC * D].rearrange("p (f d) -> p f d", f=FC)
        sdn_lo = second_lo[:, 0:FC * D].rearrange("p (f d) -> p f d", f=FC)
        wout_hi = second_hi[:, FC * D:(FC + KC) * D].rearrange("p (c d) -> p c d", c=KC)
        wout_lo = second_lo[:, FC * D:(FC + KC) * D].rearrange("p (c d) -> p c d", c=KC)
        h_sb = sgu[:, 0, :].rearrange("p (b t) -> p b t", b=2)
        act_sb = rz
        silu_sb = [early[:, 2 * D:].rearrange("p (b t) -> p b t", b=2), rz]
        rspread = ksum
        y_tok = q_sb[:, :, :].rearrange("p c (j d) -> p (c j) d", d=D)

        ps = ctx.enter_context(nc.psum_tensor("ps", [P, 8, 512], F32))
        ROUTE = 6
        logit_ps = ps[:, ROUTE, 0:NT * 2 * E].rearrange("p (i h e) -> p h e i", h=2, e=E)
        rank_ps = ps[:, ROUTE, 128:128 + NT * E]
        count_ps = ps[:, ROUTE, 192:192 + NT * E]

        s_x = [sem(f"s_x{n}") for n in range(2 * NH)]
        s_router = sem("s_router")
        s_dec = sem("s_dec")
        s_wqkv = sem("s_wqkv")
        s_wout = sem("s_wout")
        s_sgu = sem("s_sgu")
        s_sdn = sem("s_sdn")
        s_gu = [sem(f"s_gu{p}") for p in range(2)]
        s_dn = [sem(f"s_dn{p}") for p in range(2)]
        s_zero = sem("s_zero")
        s_const = sem("s_const")
        s_ve = sem("s_ve")
        s_sd = sem("s_sd")
        s_rstd = sem("s_rstd")
        s_xn = sem("s_xn")
        s_xna = sem("s_xna")
        s_xT = sem("s_xT")
        s_rT = sem("s_rT")
        s_rhi = sem("s_rhi")
        s_rlo = sem("s_rlo")
        s_xhi = sem("s_xhi")
        s_xlo = sem("s_xlo")
        s_logit = sem("s_logit")
        s_top = sem("s_top")
        s_gexp = sem("s_gexp")
        s_chosen = sem("s_chosen")
        s_rank = sem("s_rank")
        s_slot = sem("s_slot")
        s_plan = sem("s_plan")
        s_xs = sem("s_xs")
        s_scatter = sem("s_scatter")
        s_whk = sem("s_whk")
        s_whi = sem("s_whi")
        s_wlo = sem("s_wlo")
        s_dece = sem("s_dece")
        s_dech = sem("s_dech")
        s_decp = sem("s_decp")
        s_qkv = sem("s_qkv")
        s_er = sem("s_er")
        s_kv = sem("s_kv")
        s_q = sem("s_q")
        s_qmin = sem("s_qmin")
        s_qk = sem("s_qk")
        s_den = sem("s_den")
        s_rden = sem("s_rden")
        s_rdT = sem("s_rdT")
        s_rdTc = sem("s_rdTc")
        s_rdram = sem("s_rdram")
        s_spread = sem("s_spread")
        s_att = sem("s_att")
        s_atth = sem("s_atth")
        s_attl = sem("s_attl")
        s_shi = sem("s_shi")
        s_slo = sem("s_slo")
        s_phi = sem("s_phi")
        s_plo = sem("s_plo")
        s_sg = sem("s_sg")
        s_ss = sem("s_ss")
        s_sh = sem("s_sh")
        s_shh = sem("s_shh")
        s_shl = sem("s_shl")
        s_xg0 = sem("s_xg0")
        s_xg = sem("s_xg")
        s_xgT = sem("s_xgT")
        s_xgc = sem("s_xgc")
        s_gup = sem("s_gup")
        s_silu = sem("s_silu")
        s_hr = sem("s_hr")
        s_down = sem("s_down")
        s_yT = sem("s_yT")
        s_yback = sem("s_yback")
        s_yrow = sem("s_yrow")
        s_ystore = sem("s_ystore")
        s_stored = sem("s_stored")
        s_gather = sem("s_gather")
        s_acc = sem("s_acc")
        s_sum = sem("s_sum")
        s_fin = sem("s_fin")
        s_out = sem("s_out")
        s_dve = sem("s_dve")

        block = ctx.enter_context(nc.Block())

        gu_dram = w_gate_up.rearrange("e (c p) n -> e p c n", p=P)
        dn_dram = w_down.rearrange("e (c p) n -> e p c n", p=P)

        gate_bank = [4, 0, 2, 4] + [2, 0, 4, 2]

        def three(o, w_hi, w_lo, m_hi, m_lo, start, stop):
            nc.tensor.matmul(o, w_hi, m_hi, start=start, stop=False)
            nc.tensor.matmul(o, w_hi, m_lo, start=False, stop=False)
            return nc.tensor.matmul(o, w_lo, m_hi, start=False, stop=stop)

        @block.sync
        def _(sp):
            for n in range(2 * NH):
                two = slice(2 * n, 2 * n + 2)
                sp.dma_start(x_sb[:, two, :], x_rows[:, two, :]).then_inc(s_x[n], 16)
            sp.dma_start(router[:, :], router_w).then_inc(s_router, 16)
            sp.dma_start(dec_in[:, :], decay_param.rearrange("(h o) -> h o", o=1)).then_inc(s_dec, 16)
            sp.dma_start(wqkv[:, :, :], w_qkv.rearrange("(c p) n -> p c n", p=P)).then_inc(s_wqkv, 16)
            sp.wait_ge(s_wqkv, 16)
            sp.dma_start(sgu[:, :, :], shared_gate_up.rearrange("(c p) n -> p c n", p=P)).then_inc(s_sgu, 16)
            sp.wait_ge(s_const, 1)
            sp.dma_start(sorted_rows.rearrange("r d -> (r d)").rearrange("(p k w) -> p k w", p=P, k=ZK),
                         zeros[:, :].unsqueeze(1).broadcast_to([P, ZK, ZW])).then_inc(s_zero, 16)
            sp.dma_start(sdn[:, :, :], shared_down.rearrange("(c p) n -> p c n", p=P)).then_inc(s_sdn, 16)
            sp.dma_start(wout[:, :, :], w_out.rearrange("(c p) n -> p c n", p=P)).then_inc(s_wout, 16)
            for e in range(2):
                sp.dma_start(gu[e][:, :, :], gu_dram[e]).then_inc(s_gu[e], 16)
                sp.dma_start(dn[e][:, :, :], dn_dram[e]).then_inc(s_dn[e], 16)
            def refill(i, p):
                done = sp.value_load(plan[0:1, bass.ds(2 * i + p, 1)], min_val=1, max_val=TILES)
                sp.wait_ge(s_gup, 2 * done)
                sp.dma_start(gu[p][:, :, :], gu_dram[bass.ds(2 * i + (p + 2), 1)].rearrange("e p c n -> p (e c) n")).then_inc(s_gu[p], 16)
                sp.wait_ge(s_down, done)
                sp.dma_start(dn[p][:, :, :], dn_dram[bass.ds(2 * i + (p + 2), 1)].rearrange("e p c n -> p (e c) n")).then_inc(s_dn[p], 16)

            sp.wait_ge(s_scatter, 16 * NT)
            sp.wait_ge(s_wlo, 3)
            sp.dma_start(xg, sorted_rows[SLOTS:2 * SLOTS, :].rearrange("(j p) d -> p j d", p=HS)).then_inc(s_xg0, 16)
            sp.wait_ge(s_rdTc, 1)
            sp.dma_start(rden_rows.rearrange("(q d) t -> q d t", d=HD), rdT[:, :].unsqueeze(1).broadcast_to([NT * HEADS, HD, P])).then_inc(s_rdram, 16)
            sp.wait_ge(s_plan, 1)
            with sp.Fori(0, E // 2 - 1) as i:
                for p in range(2):
                    refill(i, p)
            sp.wait_ge(s_rdram, 16)
            for c in range(KC):
                sp.dma_start(rspread[:, c, :].rearrange("p (i t) -> p i t", i=NT),
                             rden_rows.rearrange("(i c p) t -> c p i t", c=KC, p=P)[c]).then_inc(s_spread, 16)
            for i in range(NT):
                sp.wait_ge(s_fin, i + 1)
                sp.dma_start(out_rows[:, i, :], x_sb[:, i, :]).then_inc(s_out, 16)
            sp.wait_ge(s_out, 16 * NT)

        @block.gpsimd
        def _(pool):
            pool.memset(zeros[:, :], 0.0).then_inc(s_const, 1)
            pool.memset(ident[:, :], 0.0).then_inc(s_const, 1)
            pool.memset(ones[:, :], 1.0).then_inc(s_const, 1)
            pool.memset(head_of[:, :], 1.0).then_inc(s_const, 1)
            pool.memset(spread[:, :, :], 1.0).then_inc(s_const, 1)
            pool.wait_ge(s_const, 5)
            pool.affine_select(out=ident[:, :], in_=ident[:, :], compare_op=ALU.not_equal, fill=1.0,
                               base=0, pattern=[[-1, P]], channel_multiplier=1).then_inc(s_const, 1)
            pool.affine_select(out=before[:, :], in_=ones[:, :], compare_op=ALU.is_gt, fill=0.0,
                               base=0, pattern=[[1, P]], channel_multiplier=-1).then_inc(s_const, 1)
            pool.affine_select(out=head_of[:, :], in_=head_of[:, :], compare_op=ALU.is_ge, fill=0.0,
                               base=0, pattern=[[-HD, HC]], channel_multiplier=1).then_inc(s_const, 1)
            pool.affine_select(out=spread[:, :, :], in_=spread[:, :, :], compare_op=ALU.is_ge, fill=0.0,
                               base=0, pattern=[[P, KC], [1, P]], channel_multiplier=-HD).then_inc(s_const, 1)
            pool.wait_ge(s_const, 9)
            pool.affine_select(out=head_of[:, :], in_=head_of[:, :], compare_op=ALU.is_ge, fill=0.0,
                               base=HD - 1, pattern=[[HD, HC]], channel_multiplier=-1).then_inc(s_const, 1)
            pool.affine_select(out=spread[:, :, :], in_=spread[:, :, :], compare_op=ALU.is_ge, fill=0.0,
                               base=HD - 1, pattern=[[-P, KC], [-1, P]], channel_multiplier=HD).then_inc(s_const, 1)
            pool.iota(em_int[:, :], pattern=[[1, E]], base=-E, channel_multiplier=0).then_inc(s_const, 1)
            pool.iota(steps_int[:, :, :], pattern=[[0, E], [SLOTS, STEPS]], base=SLOTS,
                      channel_multiplier=0).then_inc(s_const, 1)
            pool.memset(restart[:, :, :], 1.0).then_inc(s_const, 1)
            pool.memset(ones8[:, :], 1.0).then_inc(s_const, 1)
            pool.memset(yT[:, :, :], 0.0).then_inc(s_yT, 1)
            pool.memset(yrow[:, :, :], 0.0).then_inc(s_yrow, 1)
            pool.wait_ge(s_const, 15)
            pool.memset(restart[:, :, 0:1], 0.0).then_inc(s_const, 1)
            pool.tensor_copy(em[:, :], em_int[:, :]).then_inc(s_const, 1)
            pool.tensor_copy(steps[:, :, :], steps_int[:, :, :]).then_inc(s_const, 1)
            for k, j in enumerate((1, 2, 0)):
                if k == 0:
                    pool.wait_ge(s_whk, 1)
                else:
                    pool.wait_ge(s_whi, k)
                cols = slice(j * D, (j + 1) * D)
                pool.tensor_tensor(wqkv_lo[:, :, cols], wqkv[:, :, cols], wqkv_hi[:, :, cols].bitcast(F32), ALU.subtract).then_inc(s_wlo, 1)
            for k in range(4):
                pool.wait_ge(s_shi, k + 1)
                c, cols = k // 2, slice((k % 2) * F, (k % 2 + 1) * F)
                pool.tensor_tensor(sgu_lo[:, c, cols], sgu[:, c, cols], sgu_hi[:, c, cols].bitcast(F32), ALU.subtract).then_inc(s_slo, 1)
            pool.wait_ge(s_zero, 16)
            pool.wait_ge(s_yrow, 1)
            pool.dma_start(sorted_rows[0:SLOTS, :].rearrange("(j p) d -> p j d", p=HS), yrow[:, :, :]).then_inc(s_ystore, 16)
            n, c = 0, 1
            pool.wait_ge(s_er, 4)
            pool.tensor_scalar(ez[:, 1, :], ez[:, 1, :], 1.0, None, ALU.min).then_inc(s_qmin, 1)
            pool.wait_ge(s_qmin, 1)
            pool.tensor_tensor(q_sb[:, c, n * 512:(n + 1) * 512], ez[:, 1, :], rz[:, 1, :], ALU.add).then_inc(s_q, 1)

            pool.wait_ge(s_slot, 1)
            pool.wait_ge(s_ystore, 16)
            for i in range(NT):
                pool.wait_ge(s_xs, i + 1)
                pool.indirect_dma_start(sorted_rows, bass.IndirectOffsetOnAxis(ap=slot_row[:, i:i + 1], axis=0),
                                        xn[:, i, :], None).then_inc(s_scatter, 16)
            pool.wait_ge(s_phi, 2)
            pool.tensor_tensor(wout_lo, wout[:, :, :], wout_hi.bitcast(F32), ALU.subtract).then_inc(s_plo, 1)
            pool.wait_ge(s_plan, 1)
            total = pool.value_load(plan[0:1, E - 1:E], min_val=E, max_val=TILES)
            with pool.Fori(0, total) as t:
                pool.wait_ge(s_xgT, t + 1)
                pool.dma_start(xg, sorted_rows[bass.ds(t * SLOTS + 2 * SLOTS, SLOTS), :].rearrange("(j p) d -> p j d", p=HS)).then_inc(s_xg, 16)
                pool.wait_ge(s_yrow, t + 2)
                pool.dma_start(sorted_rows[bass.ds(t * SLOTS, SLOTS), :].rearrange("(j p) d -> p j d", p=HS), yrow[:, :, :]).then_inc(s_ystore, 16)
            pool.wait_ge(s_yrow, total + 2)
            pool.dma_start(sorted_rows[bass.ds(total * SLOTS, SLOTS), :].rearrange("(j p) d -> p j d", p=HS), yrow[:, :, :]).then_inc(s_ystore, 16)
            pool.wait_ge(s_ystore, 16 * total + 32)
            pool.sem_inc(s_stored, 1)
            pool.wait_ge(s_stored, 1)
            for i in range(NT):
                pool.indirect_dma_start(y_tok[:, i, :], None, sorted_rows,
                                        bass.IndirectOffsetOnAxis(ap=slot_row[:, i:i + 1], axis=0)).then_inc(s_gather, 16)
            pool.wait_ge(s_gather, 16 * NT)
            pool.wait_ge(s_xg, 16 * total)

        @block.scalar
        def _(act):
            A = nc.scalar.activation

            def norm(n):
                act.wait_ge(s_rstd, n + 1)
                for i in (n * TH + 2, n * TH + 3):
                    A(xn[:, i, :], x_sb[:, i, :], ACT.Identity, scale=rstd[:, i:i + 1], bias=shift[:, i:i + 1]).then_inc(s_xna, 1)

            def x_hi(n):
                act.wait_ge(s_xT, TH * (n + 1))
                for c in range(KC):
                    A(xT_hi[:, c, n * 512:(n + 1) * 512], ps[:, 4 + c, :], ACT.Copy).then_inc(s_xhi, 1)

            act.wait_ge(s_ve, 1)
            A(sd[:, 0:TH], ve[:, 0:TH], ACT.Sqrt).then_inc(s_sd, 1)
            norm(0)
            act.wait_ge(s_rT, 1)
            A(rT[:, :, 0, :], ps[:, 7, 0:KC * E].rearrange("p (c e) -> p c e", e=E), ACT.Copy).then_inc(s_rhi, 1)
            x_hi(0)
            act.wait_ge(s_wqkv, 16)
            for j in (2, 0):
                A(wqkv_hi[:, :, j * D:(j + 1) * D], wqkv[:, :, j * D:(j + 1) * D], ACT.Copy).then_inc(s_whi, 1)
            act.wait_ge(s_ve, 2)
            A(sd[:, TH:NT], ve[:, TH:NT], ACT.Sqrt).then_inc(s_sd, 1)
            norm(1)
            act.wait_ge(s_dec, 16)
            A(dec_e[:, :], dec_in[:, :], ACT.Exp, scale=-1.0).then_inc(s_dece, 1)

            def scale_tokens(tiles):
                act.wait_ge(s_xT, NT)
                act.wait_ge(s_slot, 1)
                for i in tiles:
                    A(xn[:, i, :], xn[:, i, :], ACT.Identity, scale=gate[:, i:i + 1]).then_inc(s_xs, 1)

            for a in range(2 * NH):
                if a == 2:
                    act.wait_ge(s_top, 1)
                    A(gexp[:, :], top[:, :], ACT.Exp, scale=-1.0).then_inc(s_gexp, 1)
                for j, t in ((0, 3 * a), (1, 3 * a + 2)):
                    act.wait_ge(s_qkv, t + 1)
                    if a >= 1:
                        act.wait_ge((s_kv, s_q)[j], a)
                    A(ez[:, j, :], ps[:, t % 4, :], ACT.Exp)
                    A(rz[:, j, :], ps[:, t % 4, :], ACT.Relu).then_inc(s_er, 1)
                    if t == 0:
                        x_hi(1)
                    if t == 3 * 3:
                        scale_tokens(range(3))
                if a == 0:
                    act.wait_ge(s_sgu, 16)
                    for c in range(KC):
                        for h in range(2):
                            A(sgu_hi[:, c, h * F:(h + 1) * F], sgu[:, c, h * F:(h + 1) * F], ACT.Copy).then_inc(s_shi, 1)

            def sorted_copy(done):
                act.wait_ge(s_xgT, done)
                A(xgT, ps[:, 4, 0:KC * SLOTS].rearrange("p (c s) -> p c s", c=KC), ACT.Copy).then_inc(s_xgc, 1)

            def shared_silu(n):
                for f in range(FC + 1):
                    k = n * FC + f
                    if f < FC:
                        act.wait_ge(s_sg, 2 * k + 1)
                        if k >= 2:
                            act.wait_ge(s_sh, k - 1)
                        A(silu_sb[n][:, k % 2, :], ps[:, gate_bank[k], :], ACT.Silu).then_inc(s_ss, 1)
                    if n == 0 and f == FC - 1:
                        act.wait_ge(s_sdn, 16)
                        A(sdn_hi, sdn[:, :, :], ACT.Copy).then_inc(s_phi, 1)
                        act.wait_ge(s_wout, 16)
                        A(wout_hi, wout[:, :, :], ACT.Copy).then_inc(s_phi, 1)
                    if n == 1 and f < KC:
                        act.wait_ge(s_att, f + 1)
                        A(att_hi[:, f, :], kvsum[:, f, :], ACT.Copy).then_inc(s_atth, 1)
                    if n == 0 and f == FC:
                        sorted_copy(1)
                        act.wait_ge(s_rdT, 1)
                        A(rdT[:, :], ps[:, 7, 0:P], ACT.Copy).then_inc(s_rdTc, 1)
                    if f >= 1:
                        act.wait_ge(s_sh, k)
                        A(hT_hi[n][:, f - 1, :], h_sb[:, (k - 1) % 2, :], ACT.Copy).then_inc(s_shh, 1)

            scale_tokens(range(3, NT))
            act.wait_ge(s_wlo, 3)
            shared_silu(0)
            act.wait_ge(s_q, 2 * NH)
            act.wait_ge(s_plan, 1)
            total = act.value_load(plan[0:1, E - 1:E], min_val=E, max_val=TILES)
            with act.Fori(0, total) as t:
                for h in range(2):
                    act.wait_ge(s_gup, 2 * t + (h + 1))
                    A(act_sb[:, h, 0:2 * SLOTS], ps[:, 2 * h, 0:2 * SLOTS], ACT.Silu).then_inc(s_silu, 1)
                sorted_copy(t + 2)
                act.wait_ge(s_down, t + 1)
                A(yT[:, :, :], ps[:, 5:7, 0:SLOTS], ACT.Copy).then_inc(s_yT, 1)
            shared_silu(1)

        @block.vector
        def _(dve):
            steps_done = [0]

            def link(ins):
                steps_done[0] += 1
                ins.then_inc(s_dve, 1)
                dve.wait_ge(s_dve, steps_done[0])

            V = nc.vector

            def statistics(i):
                if i % 2 == 0:
                    dve.wait_ge(s_x[i // 2], 16)
                return V.bn_stats(bn[:, i, :], x_sb[:, i, :])

            def variances(n):
                for i in range(n * TH, (n + 1) * TH):
                    ins = V.bn_aggr(mv[:, i, :], bn[:, i, :])
                link(ins)
                h = slice(n * TH, (n + 1) * TH)
                V.tensor_scalar(ve[:, h], mv[:, h, 1], EPS_LN, None, ALU.add).then_inc(s_ve, 1)

            def normalise(n):
                h = slice(n * TH, (n + 1) * TH)
                dve.wait_ge(s_sd, n + 1)
                link(V.reciprocal(rs[:, h], sd[:, h]))
                link(V.tensor_tensor(rt[:, h], rs[:, h], rs[:, h], ALU.mult))
                link(V.tensor_tensor(rt[:, h], rt[:, h], ve[:, h], ALU.mult))
                link(V.tensor_scalar(rt[:, h], rt[:, h], -0.5, 1.5, ALU.mult, ALU.add))
                link(V.tensor_tensor(rstd[:, h], rs[:, h], rt[:, h], ALU.mult))
                V.scalar_tensor_tensor(shift[:, h], mv[:, h, 0], -1.0, rstd[:, h], ALU.mult, ALU.mult).then_inc(s_rstd, 1)
                for i in (n * TH, n * TH + 1):
                    V.tensor_scalar(xn[:, i, :], x_sb[:, i, :], mv[:, i, 0:1], rstd[:, i:i + 1], ALU.subtract, ALU.mult).then_inc(s_xn, 1)

            def x_lo(n):
                cols = slice(n * 512, (n + 1) * 512)
                for c in range(KC):
                    dve.wait_ge(s_xhi, 2 * n + c + 1)
                    V.tensor_tensor(xT_lo[:, c, cols], ps[:, 4 + c, :], xT_hi[:, c, cols].bitcast(F32), ALU.subtract).then_inc(s_xlo, 1)

            em_b = em[:, :].unsqueeze(2).broadcast_to([P, E, NT])
            flat = "p e i -> p (e i)"

            def choose():
                dve.wait_ge(s_logit, 1)
                link(V.tensor_copy(low_logits[:, :, :], logit_ps[:, 1, :, :]))
                link(V.tensor_tensor(logits[:, :, :], low_logits[:, :, :], logit_ps[:, 0, :, :], ALU.add))
                V.tensor_reduce(top[:, :], logits[:, :, :].rearrange("p e i -> p i e"), AX.X, ALU.max).then_inc(s_top, 1)
                dve.wait_ge(s_top, 1)
                link(V.tensor_tensor(is_top[:, :, :], logits[:, :, :], top[:, :].unsqueeze(1).broadcast_to([P, E, NT]), ALU.is_equal))
                dve.wait_ge(s_const, 18)
                link(V.tensor_tensor(cand[:, :, :], is_top[:, :, :], em_b, ALU.mult))
                link(V.tensor_reduce(first[:, :], cand[:, :, :].rearrange("p e i -> p i e"), AX.X, ALU.min))
                V.tensor_tensor(chosen[:, :, :], em_b, first[:, :].unsqueeze(1).broadcast_to([P, E, NT]), ALU.is_equal).then_inc(s_chosen, 1)

            def place():
                dve.wait_ge(s_rank, 1)
                link(V.tensor_tensor_scan(upto[:, :, :].rearrange(flat), restart[:, :, :].rearrange(flat), count_ps, 0.0, ALU.mult, ALU.add))
                link(V.tensor_tensor(pos[:, :, :].rearrange(flat), upto[:, :, :].rearrange(flat), count_ps, ALU.subtract))
                link(V.tensor_tensor(pos[:, :, :].rearrange(flat), pos[:, :, :].rearrange(flat), rank_ps, ALU.add))
                link(V.tensor_tensor(over[:, :, :], upto[:, :, NT - 1:NT].broadcast_to([P, E, STEPS]), steps[:, :, :], ALU.is_gt))
                link(V.tensor_reduce(tiles_of[:, :], over[:, :, :], AX.X, ALU.add))
                link(V.tensor_scalar(tiles_one[:, :], tiles_of[:, :], 1.0, None, ALU.add))
                link(V.tensor_tensor_scan(tiles_upto[:, :], ones8[:, :], tiles_one[:, :], 0.0, ALU.mult, ALU.add))
                link(V.tensor_tensor(base[:, :], tiles_upto[:, :], tiles_one[:, :], ALU.subtract))
                link(V.scalar_tensor_tensor(pos[:, :, :], base[:, :].unsqueeze(2).broadcast_to([P, E, NT]), float(SLOTS), pos[:, :, :], ALU.mult, ALU.add))
                link(V.tensor_tensor(pos[:, :, :], pos[:, :, :], chosen[:, :, :], ALU.mult))
                link(V.tensor_reduce(slot[:, :], pos[:, :, :].rearrange("p e i -> p i e"), AX.X, ALU.add))
                dve.wait_ge(s_gexp, 1)
                link(V.tensor_scalar(gone[:, :], gexp[:, :], 1.0, None, ALU.add))
                V.reciprocal(gate[:, :], gone[:, :])
                V.tensor_scalar(slot_row[:, :], slot[:, :], float(SLOTS), None, ALU.add).then_inc(s_slot, 1)
                V.tensor_copy(plan[:, :], tiles_upto[0:1, :]).then_inc(s_plan, 1)

            for i in range(TH):
                ins = statistics(i)
            link(ins)
            variances(0)
            normalise(0)
            dve.wait_ge(s_wqkv, 16)
            V.tensor_copy(wqkv_hi[:, :, D:2 * D], wqkv[:, :, D:2 * D]).then_inc(s_whk, 1)
            dve.wait_ge(s_rhi, 1)
            V.tensor_tensor(rT[:, :, 1, :], ps[:, 7, 0:KC * E].rearrange("p (c e) -> p c e", e=E),
                            rT[:, :, 0, :].bitcast(F32), ALU.subtract).then_inc(s_rlo, 1)
            statistics(TH)
            statistics(TH + 1)
            x_lo(0)
            statistics(TH + 2)
            link(statistics(TH + 3))
            variances(1)
            normalise(1)
            dve.wait_ge(s_dece, 1)
            link(V.tensor_scalar(dec_1[:, :], dec_e[:, :], 1.0, None, ALU.add))
            V.reciprocal(dec_h[:, :], dec_1[:, :]).then_inc(s_dech, 1)
            for a in range(2 * NH):
                n, c = a // 2, a % 2
                cols = slice(n * 512, (n + 1) * 512)
                rate = decay[:, c:c + 1].broadcast_to([P, 512])
                dve.wait_ge(s_er, 2 * a + 1)
                link(V.scalar_tensor_tensor(k_sb[:, :], ez[:, 0, :], 1.0, rz[:, 0, :], ALU.min, ALU.add))
                dve.wait_ge(s_qkv, 3 * a + 2)
                V.tensor_tensor(kv_sb[:, :], k_sb[:, :], ps[:, (3 * a + 1) % 4, :], ALU.mult).then_inc(s_kv, 1)
                if a == 0:
                    x_lo(1)
                    dve.wait_ge(s_decp, 1)
                    link(V.tensor_copy(decay[:, :], ps[:, 7, 64:64 + KC]))
                if a == 1:
                    choose()
                if a == 2:
                    place()
                V.tensor_tensor_scan(ksum[:, c, cols], rate, k_sb[:, :], ksum[:, c, n * 512 - 1:n * 512] if n else 0.0, ALU.mult, ALU.add)
                dve.wait_ge(s_kv, a + 1)
                link(V.tensor_tensor_scan(kvsum[:, c, cols], rate, kv_sb[:, :], kvsum[:, c, n * 512 - 1:n * 512] if n else 0.0, ALU.mult, ALU.add))
                if a != 1:
                    dve.wait_ge(s_er, 2 * a + 2)
                    V.scalar_tensor_tensor(q_sb[:, c, cols], ez[:, 1, :], 1.0, rz[:, 1, :], ALU.min, ALU.add).then_inc(s_q, 1)

            def times_q(sums, c, n):
                cols = slice(n * 512, (n + 1) * 512)
                return V.tensor_tensor(sums[:, c, cols], q_sb[:, c, cols], sums[:, c, cols], ALU.mult)

            def shared_hidden(n, f):
                k = n * FC + f
                if f < FC:
                    dve.wait_ge(s_ss, k + 1)
                    dve.wait_ge(s_sg, 2 * k + 2)
                    if k >= 2:
                        dve.wait_ge(s_shl, k - 1)
                    V.tensor_tensor(h_sb[:, k % 2, :], silu_sb[n][:, k % 2, :], ps[:, gate_bank[k] + 1, :], ALU.mult).then_inc(s_sh, 1)
                if f >= 1:
                    dve.wait_ge(s_shh, k)
                    V.tensor_tensor(hT_lo[n][:, f - 1, :], h_sb[:, (k - 1) % 2, :], hT_hi[n][:, f - 1, :].bitcast(F32), ALU.subtract).then_inc(s_shl, 1)

            dve.wait_ge(s_slo, 4)
            dve.wait_ge(s_q, 2 * NH)
            for c in range(KC):
                times_q(ksum, c, 0).then_inc(s_qk, 1)
            shared_hidden(0, 0)
            for c in range(KC):
                times_q(ksum, c, 1).then_inc(s_qk, 1)
            for f in range(1, FC):
                shared_hidden(0, f)
                if f == KC:
                    dve.wait_ge(s_den, 1)
                    link(V.tensor_scalar(den[:, :], ps[:, ROUTE, 0:NT * HEADS], EPS_DEN, None, ALU.max))
                    V.reciprocal(rden[:, :], den[:, :]).then_inc(s_rden, 1)
                if f <= KC:
                    for n in range(NH):
                        ins = times_q(kvsum, f - 1, n)
                    link(ins)
            shared_hidden(0, FC)
            dve.wait_ge(s_phi, 2)
            V.tensor_tensor(sdn_lo, sdn[:, :, :], sdn_hi.bitcast(F32), ALU.subtract).then_inc(s_plo, 1)

            def rows_copy(t):
                dve.wait_ge(s_yback, t + 1)
                dve.wait_ge(s_ystore, 16 * t + 16)
                V.tensor_copy(yrow[:, :, :].rearrange("p j d -> p (j d)"), ps[0:HS, 7, :]).then_inc(s_yrow, 1)

            dve.wait_ge(s_plan, 1)
            total = dve.value_load(plan[0:1, E - 1:E], min_val=E, max_val=TILES)
            with dve.Fori(0, total) as t:
                for h in range(2):
                    dve.wait_ge(s_silu, 2 * t + (h + 1))
                    V.tensor_tensor(hr[:, 2 * h:2 * h + 2, :].rearrange("p f s -> p (f s)"), act_sb[:, h, 0:2 * SLOTS],
                                    ps[:, 2 * h + 1, 0:2 * SLOTS], ALU.mult).then_inc(s_hr, 1)
                    if h == 0:
                        rows_copy(t)
            rows_copy(total)
            dve.wait_ge(s_spread, 16 * KC)
            for c in range(KC):
                V.tensor_tensor(kvsum[:, c, :], kvsum[:, c, :], rspread[:, c, :], ALU.mult).then_inc(s_att, 1)
            for f in range(FC + 1):
                shared_hidden(1, f)
                if f < KC:
                    dve.wait_ge(s_atth, f + 1)
                    V.tensor_tensor(att_lo[:, f, :], kvsum[:, f, :], att_hi[:, f, :].bitcast(F32), ALU.subtract).then_inc(s_attl, 1)
            for i in range(TH):
                dve.wait_ge(s_acc, i + 1)
                V.tensor_tensor(x_sb[:, i, :], x_sb[:, i, :], ps[:, 4 + i, 0:D], ALU.add).then_inc(s_sum, 1)
            dve.wait_ge(s_gather, 16 * NT)
            for i in range(NT):
                if i < TH:
                    dve.wait_ge(s_sum, i + 1)
                V.tensor_tensor(x_sb[:, i, :], x_sb[:, i, :], y_tok[:, i, :], ALU.add).then_inc(s_fin if i < TH else s_sum, 1)
            for i in range(TH, NT):
                dve.wait_ge(s_acc, i + 1)
                dve.wait_ge(s_sum, i + 1)
                V.tensor_tensor(x_sb[:, i, :], x_sb[:, i, :], ps[:, 4 + i % TH, 0:D], ALU.add).then_inc(s_fin, 1)

        @block.tensor
        def _(pe):
            mm = nc.tensor.matmul
            tr = nc.tensor.transpose

            def transpose_tokens(n):
                for j in range(TH):
                    i = n * TH + j
                    if j < 2:
                        pe.wait_ge(s_xn, 2 * n + j + 1)
                    else:
                        pe.wait_ge(s_xna, 2 * n + j - 1)
                    if n and j == 0:
                        pe.wait_ge(s_xlo, 2)
                    for c in range(KC):
                        ins = tr(ps[:, 4 + c, j * P:(j + 1) * P], xn[:, i, c * P:(c + 1) * P], ident[:, :])
                    ins.then_inc(s_xT, 1)

            def router_logits(n):
                pe.wait_ge(s_rlo, 1)
                pe.wait_ge(s_xlo, 2 * n + 2)
                for i in range(n * TH, (n + 1) * TH):
                    cols = slice(i * P, (i + 1) * P)
                    both = ps[:, ROUTE, i * 2 * E:(i + 1) * 2 * E]
                    mm(both, xT_hi[:, 0, cols], rT[:, 0, :, :].rearrange("p h e -> p (h e)"), start=True, stop=False)
                    for c in range(KC):
                        mm(both[:, 0:E], xT_lo[:, c, cols], rT[:, c, 0, :], start=False, stop=False, skip_group_check=True)
                    ins = mm(both, xT_hi[:, 1, cols], rT[:, 1, :, :].rearrange("p h e -> p (h e)"), start=False, stop=True)
                if n:
                    ins.then_inc(s_logit, 1)

            def ranks():
                pe.wait_ge(s_chosen, 1)
                pick = chosen[:, :, :].rearrange("p e i -> p (e i)")
                mm(rank_ps, before[:, :], pick, start=True, stop=True)
                mm(count_ps, ones[:, :], pick, start=True, stop=True).then_inc(s_rank, 1)

            def qkv_tile(t):
                a, j = t // 3, (1, 2, 0)[t % 3]
                n, c = a // 2, a % 2
                if t == 0:
                    pe.wait_ge(s_whk, 1)
                else:
                    if t < 3:
                        pe.wait_ge(s_whi, t)
                    pe.wait_ge(s_xlo, 2 * n + 2)
                if t >= 4:
                    u = t - 4
                    if u % 3 == 1:
                        pe.wait_ge(s_kv, u // 3 + 1)
                    else:
                        pe.wait_ge(s_er, 2 * (u // 3) + (1 if u % 3 == 0 else 2))
                rows = slice(n * 512, (n + 1) * 512)
                cols = slice(j * D + c * P, j * D + (c + 1) * P)
                o = ps[:, t % 4, :]
                def hi_hi():
                    for kc in range(KC):
                        if t == 0:
                            pe.wait_ge(s_xhi, kc + 1)
                        mm(o, wqkv_hi[:, kc, cols], xT_hi[:, kc, rows], start=(kc == 0), stop=False)

                def hi_lo(last):
                    for kc in range(KC):
                        if t == 0:
                            pe.wait_ge(s_xlo, kc + 1)
                        ins = mm(o, wqkv_hi[:, kc, cols], xT_lo[:, kc, rows], start=False, stop=last and kc == KC - 1)
                    return ins

                def lo_hi(last):
                    if t < 3:
                        pe.wait_ge(s_wlo, t + 1)
                    for kc in range(KC):
                        ins = mm(o, wqkv_lo[:, kc, cols], xT_hi[:, kc, rows], start=False, stop=last and kc == KC - 1)
                    return ins

                hi_hi()
                if t == 0:
                    lo_hi(False)
                    ins = hi_lo(True)
                else:
                    hi_lo(False)
                    ins = lo_hi(True)
                ins.then_inc(s_qkv, 1)

            def shared_tile(n, f, u, total=None):
                k = n * FC + f
                if k == 0:
                    pe.wait_ge(s_slo, 3 + u)
                if k == 1 and u == 0:
                    pe.wait_ge(s_er, 4 * NH - 1)
                if k == 2 and u == 0:
                    pe.wait_ge(s_er, 4 * NH)
                    pe.wait_ge(s_kv, 2 * NH)
                if f == 3:
                    pe.wait_ge((s_ss, s_sh)[u], k - 2)
                if k == 6 and u == 0:
                    pe.wait_ge(s_xgc, total + 1)
                    pe.wait_ge(s_yT, total + 1)
                for kc in range(KC):
                    col = u * F + f * P
                    ins = three(ps[:, gate_bank[k] + u, :], sgu_hi[:, kc, col:col + P], sgu_lo[:, kc, col:col + P],
                                xT_hi[:, kc, n * 512:(n + 1) * 512], xT_lo[:, kc, n * 512:(n + 1) * 512], kc == 0, kc == KC - 1)
                ins.then_inc(s_sg, 1)

            def denominators(tiles):
                pe.wait_ge(s_qk, KC * (max(tiles) // TH + 1))
                for i in tiles:
                    for c in range(KC):
                        col = i * HEADS + c * HC
                        ins = mm(ps[:, ROUTE, col:col + HC], ksum[:, c, i * P:(i + 1) * P], head_of[:, :], start=True, stop=True)
                return ins

            def transpose_sorted(s_load, loaded):
                pe.wait_ge(s_load, loaded)
                for c in range(KC):
                    for j in range(2):
                        col = c * SLOTS + j * HS
                        ins = tr(ps[:, 4, col:col + HS], xg[:, j, c * P:(c + 1) * P], ident[0:HS, 0:HS])
                ins.then_inc(s_xgT, 1)

            def transpose_back(copied):
                pe.wait_ge(s_yT, copied)
                for c in range(KC):
                    for j in range(2):
                        ins = tr(ps[0:HS, 7, j * D + c * P:j * D + (c + 1) * P], yT[:, c, j * HS:(j + 1) * HS], ident[:, :])
                ins.then_inc(s_yback, 1)

            pe.wait_ge(s_const, 3)
            with pe.Fori(0, WARM) as _i:
                mm(ps[:, 0, :], ones[:, :], ones[:, :].unsqueeze(1).broadcast_to([P, 4, P]), start=True, stop=True)
            pe.wait_ge(s_const, 11)
            pe.wait_ge(s_router, 16)
            for c in range(KC):
                ins = tr(ps[:, 7, c * E:(c + 1) * E], router[:, c * P:(c + 1) * P], ident[0:E, 0:E])
            ins.then_inc(s_rT, 1)
            transpose_tokens(0)
            for t in range(4):
                qkv_tile(t)
            transpose_tokens(1)
            router_logits(0)
            pe.wait_ge(s_dech, 1)
            for c in range(KC):
                ins = mm(ps[:, 7, 64 + c:65 + c], spread[:, c, :], dec_h[:, :], start=True, stop=True)
            ins.then_inc(s_decp, 1)
            for t in range(4, 6):
                qkv_tile(t)
            router_logits(1)
            for t in range(6, 9):
                qkv_tile(t)
            ranks()
            for t in range(9, 12):
                qkv_tile(t)
            ends = []

            def read_end():
                e = len(ends)
                ends.append(pe.value_load(plan[0:1, e:e + 1], min_val=e + 1, max_val=TILES))

            for f in range(FC):
                for u in range(2):
                    shared_tile(0, f, u)
                    if f == 0 and u == 0:
                        pe.wait_ge(s_plan, 1)
                    read_end()
                    if (f, u) == (2, 1):
                        denominators(range(3))
                    if (f, u) == (3, 0):
                        denominators(range(3, NT)).then_inc(s_den, 1)
            pe.wait_ge(s_ss, FC)
            transpose_sorted(s_xg0, 16)
            pe.wait_ge(s_rden, 1)
            tr(ps[:, 7, 0:P], rden[:, :], ident[:, :]).then_inc(s_rdT, 1)
            pe.wait_ge(s_sh, FC - 1)
            for e in range(E):
                p = e % 2
                pe.wait_ge(s_gu[p], 16 * (e // 2) + 16)
                with pe.Fori(ends[e - 1] if e else 0, ends[e]) as t:
                    pe.wait_ge(s_xgc, t + 1)
                    for h in range(2):
                        for u in range(2):
                            for f in (2 * h, 2 * h + 1):
                                for kc in range(KC):
                                    col = u * F + f * P
                                    ins = mm(ps[:, 2 * h + u, (f % 2) * SLOTS:(f % 2 + 1) * SLOTS],
                                             gu[p][:, kc, col:col + P], xgT[:, kc, :], start=(kc == 0), stop=(kc == KC - 1))
                        ins.then_inc(s_gup, 1)
                        if h == 0:
                            if e == 0:
                                pe.wait_ge(s_rdTc, 1)
                            pe.wait_ge(s_yrow, t + 1)
                            transpose_back(t + 1)
                    transpose_sorted(s_xg, 16 * t + 16)
                    if e == 0:
                        pe.wait_ge(s_sh, FC)
                    pe.wait_ge(s_dn[p], 16 * (e // 2) + 16)
                    for h in range(2):
                        pe.wait_ge(s_hr, 2 * t + (h + 1))
                        for c in range(KC):
                            for f in (2 * h, 2 * h + 1):
                                ins = mm(ps[:, 5 + c, 0:SLOTS], dn[p][:, f, c * P:(c + 1) * P], hr[:, f, :],
                                         start=(f == 0), stop=(f == FC - 1))
                    ins.then_inc(s_down, 1)

            total = ends[E - 1]
            pe.wait_ge(s_yrow, total + 1)
            shared_tile(1, 0, 0)
            transpose_back(total + 1)
            shared_tile(1, 0, 1)
            for f in range(1, FC):
                for u in range(2):
                    shared_tile(1, f, u, total)

            def finish(n):
                for i in range(n * TH, (n + 1) * TH):
                    j = i % TH
                    if n:
                        pe.wait_ge(s_sum, i - TH + 1)
                    rows = slice(j * P, (j + 1) * P)
                    o = ps[:, 4 + j, 0:D]
                    for f in range(FC):
                        three(o, hT_hi[n][:, f, rows], hT_lo[n][:, f, rows], sdn_hi[:, f, :], sdn_lo[:, f, :], f == 0, False)
                    rows = slice(i * P, (i + 1) * P)
                    for c in range(KC):
                        ins = three(o, att_hi[:, c, rows], att_lo[:, c, rows], wout_hi[:, c, :], wout_lo[:, c, :], False, c == KC - 1)
                    ins.then_inc(s_acc, 1)

            pe.wait_ge(s_shl, FC)
            pe.wait_ge(s_plo, 2)
            pe.wait_ge(s_attl, KC)
            pe.wait_ge(s_ss, 2 * FC - 1)
            pe.wait_ge(s_sh, 2 * FC - 1)
            pe.wait_ge(s_yrow, total + 2)
            finish(0)
            pe.wait_ge(s_shl, 2 * FC)
            finish(1)

_INS = ['L0_attn_x', 'L0_attn_w_qkv', 'L0_attn_w_out', 'L0_attn_decay_param', 'L0_ffn_router_w', 'L0_ffn_w_gate_up',
        'L0_ffn_w_down', 'L0_ffn_shared_gate_up', 'L0_ffn_shared_down']
_OUTS = [((1, 1024, 256), 'float32')]


def kernel(**inputs):
    import numpy as _np
    import concourse.bacc as _bacc
    from concourse import mybir as _mybir
    from concourse.bass_utils import run_bass_kernel_spmd as _run

    nc = _bacc.Bacc("TRN2", target_bir_lowering=False, num_devices=1)
    arrays, args = {}, []
    for name in _INS:
        a = _np.ascontiguousarray(inputs[name])
        arrays[f"in_{name}_dram"] = a
        args.append(nc.dram_tensor(f"in_{name}_dram", a.shape, _mybir.dt.from_np(a.dtype), kind="ExternalInput").ap())
    for i, (shape, dtype) in enumerate(_OUTS):
        dt = _mybir.dt.from_np(_np.dtype(dtype))
        args.append(nc.dram_tensor(f"out_{i}_dram", shape, dt, kind="ExternalOutput").ap())
    build(nc, *args)
    r = _run(nc, [arrays], core_ids=[0])
    return r.results[0]["out_0_dram"]
```
